# Optimizing a Trainium2 kernel written in Bass

```python
import numpy as np
import jax
import jax.numpy as jnp

def _softmax(x, axis=-1):
    return jax.nn.softmax(x, axis=axis)

def _gelu(x):
    return jax.nn.gelu(x, approximate=True)

def _silu(x):
    return jax.nn.silu(x)

def _sigmoid(x):
    return jax.nn.sigmoid(x)

def _layernorm(x, axis=-1, eps=1e-05):
    m = jnp.mean(x, axis=axis, keepdims=True)
    v = jnp.var(x, axis=axis, keepdims=True)
    return (x - m) / jnp.sqrt(v + eps)

def _scatter_add(tgt, idx, src, axis=0):
    return tgt.at[idx].add(src)

def _segment_sum(src, seg, n):
    return jax.ops.segment_sum(src, seg, n)
kernel_name = 'mk_decoder_preln_d1_seqx_r4_422b67'

def setup_inputs(seed: int=0):
    np.random.seed(seed)
    _w = jnp.asarray

    def _rec_inputs():
        import jax
        import jax.numpy as jnp
        _rk = jax.random.key(seed)
        x = -0.0002928 + 1 * jax.random.normal(jax.random.fold_in(_rk, 1), (8, 512, 256), jnp.float32)
        _lenS = 512 - jax.random.randint(jax.random.fold_in(_rk, 7), (8,), 0, max(1, 512 // 4) + 1, jnp.int32)
        _lenS2 = 1024 - jax.random.randint(jax.random.fold_in(_rk, 8), (8,), 0, max(1, 1024 // 4) + 1, jnp.int32)
        _ctx_1024P = jax.random.normal(jax.random.fold_in(_rk, 11), (8, 16, 256), jnp.float32)
        _ctx_1024c = jax.random.dirichlet(jax.random.fold_in(_rk, 511), 0.3 * jnp.ones((16,), jnp.float32), (8, 1024))
        _ctx_1024t = jnp.einsum('bsk,bkd->bsd', _ctx_1024c, _ctx_1024P)
        _ctx_1024t = _ctx_1024t * jax.lax.rsqrt(jnp.mean(jnp.square(_ctx_1024t)) + 1e-12) * 0.953939
        ctx_1024 = -1.78809e-06 + 0.0312453 * (_ctx_1024t + 0.3 * jax.random.normal(jax.random.fold_in(_rk, 611), (8, 1024, 256), jnp.float32))
        return (x, ctx_1024)
    x, ctx_1024 = _rec_inputs()

    def _L0_attn_setup():
        import jax, jax.numpy as jnp
        import numpy as np
        N_HEAD = 16
        EPS = 1e-06

        def _rotate_half(x):
            d = x.shape[-1] // 2
            return jnp.concatenate((-x[..., d:], x[..., :d]), axis=-1)

        def _rms_norm(x, w, eps=EPS):
            d = x.shape[-1]
            rms = jnp.linalg.norm(x, axis=-1, keepdims=True) * d ** (-0.5)
            return w * (x / (rms + eps))
        key = jax.random.key(seed)
        ks = jax.random.split(key, 3)
        B, T, C = (4, 512, 256)
        x = jax.random.normal(ks[0], (B, T, C), dtype=jnp.float32)
        W_kqv = jax.random.normal(ks[1], (3 * C, C), dtype=jnp.float32) * C ** (-0.5)
        W_proj = jax.random.normal(ks[2], (C, C), dtype=jnp.float32) * C ** (-0.5)
        D = C // N_HEAD
        q_norm_w = jnp.ones((D,), dtype=jnp.float32)
        k_norm_w = jnp.ones((D,), dtype=jnp.float32)
        return {'x': x, 'W_kqv': W_kqv, 'W_proj': W_proj, 'q_norm_w': q_norm_w, 'k_norm_w': k_norm_w}
    _L0_attn_all = _L0_attn_setup()
    _L0_attn_in = {k: v for k, v in _L0_attn_all.items() if k in ('W_kqv', 'W_proj', 'q_norm_w', 'k_norm_w')}
    del _L0_attn_all

    def _L0_xattn_setup():
        import jax, jax.numpy as jnp
        import numpy as np
        E, TPE, H, F = (64, 64, 256, 256)
        key = jax.random.key(seed)
        k1, k2, k3, k4 = jax.random.split(key, 4)
        scale = 1.0 / np.sqrt(H)
        return {'x': jax.random.normal(k1, (E, TPE, H), dtype=jnp.float32), 'w1': jax.random.normal(k2, (E, F, H), dtype=jnp.float32) * scale, 'v1': jax.random.normal(k3, (E, F, H), dtype=jnp.float32) * scale, 'w2': jax.random.normal(k4, (E, F, H), dtype=jnp.float32) * scale}
    _L0_xattn_all = _L0_xattn_setup()
    _L0_xattn_in = {k: v for k, v in _L0_xattn_all.items() if k in ()}
    del _L0_xattn_all

    def _L0_ffn_setup():
        import jax, jax.numpy as jnp
        import numpy as np
        B, S, H, E, K = (2, 256, 256, 8, 2)
        F = 4 * H
        key = jax.random.key(seed)
        ks = jax.random.split(key, 8)
        std = 0.02
        return {'x': jax.random.normal(ks[0], (B, S, H), jnp.float32), 'gate_w': jax.random.normal(ks[1], (E, H), jnp.float32) * (std / np.sqrt(H)), 'gate_bias': jnp.zeros((E,), jnp.float32), 'Wu': jax.random.normal(ks[2], (E, F, H), jnp.float32) * std, 'bu': jnp.zeros((E, F), jnp.float32), 'Wd': jax.random.normal(ks[3], (E, H, F), jnp.float32) * std, 'bd': jnp.zeros((E, H), jnp.float32), 'sWu': jax.random.normal(ks[4], (F, H), jnp.float32) * std, 'sbu': jnp.zeros((F,), jnp.float32), 'sWd': jax.random.normal(ks[5], (H, F), jnp.float32) * std, 'sbd': jnp.zeros((H,), jnp.float32)}
    _L0_ffn_all = _L0_ffn_setup()
    _L0_ffn_in = {k: v for k, v in _L0_ffn_all.items() if k in ('gate_w', 'gate_bias', 'Wu', 'bu', 'Wd', 'bd', 'sWu', 'sbu', 'sWd', 'sbd')}
    del _L0_ffn_all
    return {'x': x, 'ctx_1024': ctx_1024, 'L0_attn_W_kqv': _L0_attn_in['W_kqv'], 'L0_attn_W_proj': _L0_attn_in['W_proj'], 'L0_attn_q_norm_w': _L0_attn_in['q_norm_w'], 'L0_attn_k_norm_w': _L0_attn_in['k_norm_w'], 'L0_ffn_gate_w': _L0_ffn_in['gate_w'], 'L0_ffn_gate_bias': _L0_ffn_in['gate_bias'], 'L0_ffn_Wu': _L0_ffn_in['Wu'], 'L0_ffn_bu': _L0_ffn_in['bu'], 'L0_ffn_Wd': _L0_ffn_in['Wd'], 'L0_ffn_bd': _L0_ffn_in['bd'], 'L0_ffn_sWu': _L0_ffn_in['sWu'], 'L0_ffn_sbu': _L0_ffn_in['sbu'], 'L0_ffn_sWd': _L0_ffn_in['sWd'], 'L0_ffn_sbd': _L0_ffn_in['sbd']}

def reference(x, ctx_1024, L0_attn_W_kqv, L0_attn_W_proj, L0_attn_q_norm_w, L0_attn_k_norm_w, L0_ffn_gate_w, L0_ffn_gate_bias, L0_ffn_Wu, L0_ffn_bu, L0_ffn_Wd, L0_ffn_bd, L0_ffn_sWu, L0_ffn_sbu, L0_ffn_sWd, L0_ffn_sbd):
    import jax
    import jax.numpy as jnp

    def _L0_attn_ref(x, W_kqv, W_proj, q_norm_w, k_norm_w):
        import jax, jax.numpy as jnp
        import numpy as np
        N_HEAD = 16
        EPS = 1e-06

        def _rotate_half(x):
            d = x.shape[-1] // 2
            return jnp.concatenate((-x[..., d:], x[..., :d]), axis=-1)

        def _rms_norm(x, w, eps=EPS):
            d = x.shape[-1]
            rms = jnp.linalg.norm(x, axis=-1, keepdims=True) * d ** (-0.5)
            return w * (x / (rms + eps))
        B, T, C = x.shape
        H = N_HEAD
        D = C // H
        kqv = x @ W_kqv.T
        k, q, v = jnp.split(kqv, 3, axis=2)

        def to_heads(t):
            return t.reshape(B, T, H, D).transpose(0, 2, 1, 3)
        k, q, v = (to_heads(k), to_heads(q), to_heads(v))
        inv_freq = 1.0 / 10000.0 ** (jnp.arange(0, D, 2, dtype=jnp.float32) / D)
        t_pos = jnp.arange(T, dtype=jnp.float32)
        freqs = t_pos[:, None] * inv_freq[None, :]
        freqs = jnp.concatenate((freqs, freqs), axis=-1)
        cos = jnp.cos(freqs)[None, None]
        sin = jnp.sin(freqs)[None, None]
        q = q * cos + _rotate_half(q) * sin
        k = k * cos + _rotate_half(k) * sin
        q = _rms_norm(q, q_norm_w)
        k = _rms_norm(k, k_norm_w)
        scores = jnp.einsum('bhtd,bhsd->bhts', q, k) / jnp.sqrt(jnp.float32(D))
        causal = jnp.triu(jnp.ones((T, T), dtype=bool), k=1)
        scores = jnp.where(causal[None, None], -jnp.inf, scores)
        att = jax.nn.softmax(scores, axis=-1)
        y = jnp.einsum('bhts,bhsd->bhtd', att, v)
        y = y.transpose(0, 2, 1, 3).reshape(B, T, C)
        return y @ W_proj.T

    def _L0_xattn_ref(x, w1, v1, w2):
        import jax, jax.numpy as jnp
        import numpy as np
        E, TPE, H, F = (64, 64, 256, 256)
        h1 = jnp.einsum('eth,efh->etf', x, w1)
        h2 = jnp.einsum('eth,efh->etf', x, v1)
        g = jax.nn.gelu(h1, approximate=False) * h2
        return jnp.einsum('etf,efh->eth', g, w2)

    def _L0_ffn_ref(x, gate_w, gate_bias, Wu, bu, Wd, bd, sWu, sbu, sWd, sbd):
        import jax, jax.numpy as jnp
        import numpy as np
        B, S, H, E, K = (2, 256, 256, 8, 2)
        F = 4 * H
        b, s, h = x.shape
        x_flat = x.reshape(-1, h)
        T = x_flat.shape[0]
        scores = jax.nn.sigmoid(x_flat @ gate_w.T + gate_bias)
        top_scores, top_idx = jax.lax.top_k(scores, K)
        top_scores = top_scores / (top_scores.sum(-1, keepdims=True) + 1e-06)
        w = jnp.zeros((T, E), x.dtype).at[jnp.arange(T)[:, None], top_idx].add(top_scores)
        h1 = jnp.einsum('th,efh->etf', x_flat, Wu) + bu[:, None, :]
        a1 = jax.nn.gelu(h1, approximate=False)
        y = jnp.einsum('etf,ehf->eth', a1, Wd) + bd[:, None, :]
        combined = jnp.einsum('te,eth->th', w, y)
        sh = jax.nn.gelu(x_flat @ sWu.T + sbu, approximate=False)
        shared = (sh @ sWd.T + sbd) * 0.1
        return (combined + shared).reshape(b, s, h)
    x = x + _L0_attn_ref(_layernorm(x, axis=-1), L0_attn_W_kqv, L0_attn_W_proj, L0_attn_q_norm_w, L0_attn_k_norm_w)
    x = x + _L0_xattn_ref(_layernorm(x, axis=-1), ctx_1024, ctx_1024, ctx_1024)
    x = x + _L0_ffn_ref(_layernorm(x, axis=-1), L0_ffn_gate_w, L0_ffn_gate_bias, L0_ffn_Wu, L0_ffn_bu, L0_ffn_Wd, L0_ffn_bd, L0_ffn_sWu, L0_ffn_sbu, L0_ffn_sWd, L0_ffn_sbd)
    return x

_drawn_inputs = setup_inputs


def setup_inputs(seed=0):
    import zlib

    import numpy as np

    out = dict(_drawn_inputs(seed))
    spreads = {'L0_attn_q_norm_w': (1.0, 0.561),
     'L0_attn_k_norm_w': (1.0, 0.6),
     'L0_ffn_gate_bias': (0.0, 0.1),
     'L0_ffn_bu': (0.0, 0.8),
     'L0_ffn_bd': (0.0, 0.335),
     'L0_ffn_sbu': (0.0, 0.8),
     'L0_ffn_sbd': (0.0, 2.0)}
    factors = {'L0_ffn_gate_w': 2.879, 'L0_ffn_sWu': 8.0, 'L0_ffn_sWd': 8.0}
    for name, (base, spread) in spreads.items():
        noise = np.random.default_rng([zlib.crc32(name.encode()), seed]).standard_normal(out[name].shape)
        drawn = base * np.exp(spread * noise) if base else spread * noise
        out[name] = jnp.asarray(drawn.astype(out[name].dtype))
    for name, factor in factors.items():
        out[name] = (out[name] * factor).astype(out[name].dtype)
    return out
```

```python
from contextlib import ExitStack

import numpy as np

import concourse.bass as bass
from concourse import mybir

F32 = mybir.dt.float32
F16 = mybir.dt.float16
I32 = mybir.dt.int32
U32 = mybir.dt.uint32
ALU = mybir.AluOpType
ACT = mybir.ActivationFunctionType
AX_X = mybir.AxisListType.X

P = 128
B, T, C = 8, 512, 256
H, D = 16, 16
NT = T // P
KC = C // P
S = 1024
NF = S // P
HG = 4
NG = H // HG
E = 8
F = 1024
N = B * T
BIG = 3.0e38

PT_AT = {1: 0, 3: 384, 0: 512, 2: 1024}
PT_W = 1280
WORK = 57 * 1024
MB = 256
MT = MB // P
BLOCKS = (2 * N + E * (MB - 1)) // MB
UNROLL = 2
assert BLOCKS % UNROLL == 1
SLOTS = BLOCKS * MB


def at(b, per, count):
    return b * per + count


def decoder_kernel(nc, A, out):
    ctx = ExitStack()
    with ctx:
        def sb(name, shape, dt):
            return ctx.enter_context(nc.sbuf_tensor(name, shape, dt))

        def sem(name):
            return ctx.enter_context(nc.semaphore(name))

        def dram(name, shape, dt):
            return nc.dram_tensor(name, shape, dt, kind="Internal").ap()

        x2_dram = dram("x2_dram", (N, C), F32)
        xh_dram = dram("xh_dram", (N, 2 * C), F16)
        xt_dram = dram("xt_dram", (B, P, 2 * KC * T), F16)
        token_dram = dram("token_dram", (SLOTS, 1), F32)
        y_dram = dram("y_dram", (SLOTS, C), F32)
        res_dram = dram("res_dram", (N, C), F32)

        ps = ctx.enter_context(nc.psum_tensor("ps", [P, 8, 512], F32))

        def half(bank, n=1):
            return ps[:, bank:bank + n, :].rearrange("p b c -> p (b c)").bitcast(F16)

        weights_region = sb("weights_region", [P, 2 * 2 * E * KC * F], F16)
        work_region = sb("work_region", [P, WORK // 2], F16)

        def carver(region):
            used = [0]

            def carve(shape, dt):
                size = 4 if dt != F16 else 2
                n = int(np.prod(shape[1:])) * size // 2
                piece = region[0:shape[0], used[0]:used[0] + n]
                used[0] += n
                assert used[0] <= region.shape[1], used
                if dt != F16:
                    piece = piece.bitcast(dt)
                dims = " ".join(f"d{i}" for i in range(len(shape) - 1))
                sizes = {f"d{i}": n for i, n in enumerate(shape[1:])}
                return piece.rearrange(f"p ({dims}) -> p {dims}", **sizes) if len(shape) > 2 else piece

            return carve

        ident = sb("ident", [P, P], F32)
        identh = sb("identh", [P, P], F16)
        normw = sb("normw", [P, 2, D], F32)
        gatew = sb("gatew", [P, KC, E], F32)
        gatew_hl = sb("gatew_hl", [P, 2, KC, E], F16)
        gateb = sb("gateb", [P, E], F32)
        carve_w, carve_k = carver(weights_region), carver(work_region)
        probs = carve_w([P, 2, HG, PT_W], F32)
        carve_o = carver(weights_region)
        mask = carve_k([P, T], F32)
        cos = carve_k([P, NT, 2, D], F32)
        sin = carve_k([P, NT, 2, D], F32)
        wqkv = carve_k([P, KC, 3 * C], F32)
        wproj = carve_k([P, NG, C], F32)
        x_in = carve_k([P, NT, C], F32)
        xn = carve_k([P, NT, C], F32)
        x1 = carve_k([P, NT, C], F32)
        x2 = carve_k([P, NT, C], F32)
        minus_half = sb("minus_half", [P, 1], F32)
        plus_half = sb("plus_half", [P, 1], F32)
        stats = sb("stats", [P, NT, 6], F32)
        mv = sb("mv", [P, NT, 2], F32)
        rstd = sb("rstd", [P, NT], F32)
        xT = carve_k([P, KC, T], F32)
        qk_sb = carve_w([P, 2, 2 * C], F32)
        qk_sq = carve_w([P, 2, 2 * C], F32)
        qk_cos = carve_w([P, 2, 2 * C], F32)
        qk_sin = carve_w([P, 2, 2 * C], F32)
        qk_ss = sb("qk_ss", [P, 2, 2 * H], F32)
        aug = carve_k([P, 2, 2, H, 64], F16)
        QT = carve_w([P, H, T], F16)
        KT = carve_w([P, H // 2, T], F16)
        vaug = carve_w([P, NT, H, 32], F32)
        mx = carve_k([P, NT, H], F32)
        mx16 = carve_k([P, NG, NT, HG], F16)
        mT = carve_k([HG, 2, T], F16)
        yn = carve_w([P, NG, T], F32)
        ctx_in = carve_w([P, 2, 2048], F32)
        ctx_hi = carve_w([P, 2, 2048], F16)
        ctx_lo = carve_w([P, 2, 2048], F16)
        xT_hi = carve_k([P, KC, T], F16)
        xT_lo = carve_k([P, KC, T], F16)
        gelu = carve_o([P, 2, T], F32)
        act = carve_o([P, 2, T], F32)
        act_hi = carve_o([P, NF, T], F16)
        act_lo = carve_o([P, NF, T], F16)
        tail = carve_k([P, 4 * T], F32)
        y_sb = tail[:, 0:2 * T].rearrange("p (u t) -> p u t", u=2)
        den = tail[:, 2 * T:4 * T].rearrange("p (u t) -> p u t", u=2)
        xh = tail[:, 0:2 * T].bitcast(F16).rearrange("p (i c) -> p i c", i=NT)
        xT3 = tail[:, 2 * T:4 * T].bitcast(F16).rearrange("p (k t) -> p k t", k=2 * KC)
        logits = sb("logits", [P, B * NT, E], F32)

        ctx_rows = [t[:, 0, :].rearrange("p (f c) -> p f c", f=NF) for t in (ctx_hi, ctx_lo)]
        ctx_cols = [t[:, 1, :].rearrange("p (k f) -> p k f", k=KC) for t in (ctx_hi, ctx_lo)]

        weights = weights_region[:].rearrange("p (w h e n) -> p w h e n", w=2, h=2, e=E)
        w_shared = sb("w_shared", [P, 2, 2, KC * F], F16)
        slot_u = sb("slot_u", [P, 2, B * NT], U32)
        share = sb("share", [P, 2, B * NT], F32)
        bup = sb("bup", [P, E + 1, F // P], F32)
        block_expert = sb("block_expert", [1, BLOCKS], I32)
        tokens_u = sb("tokens_u", [P, SLOTS // P], U32)
        upper = sb("upper", [P, P], F16)
        onesh = sb("onesh", [P, P], F16)
        eights = sb("eights", [P, E], F32)
        numbers = sb("numbers", [1, BLOCKS], F32)
        carve_2 = carver(work_region)
        xt_in = carve_2([P, 2, 2 * KC, T], F16)
        stage = carve_2([P, 2, KC * F], F32)
        r_in = carve_2([P, 2, NT, C], F32)
        s_gelu = carve_2([P, 2, T], F32)
        s_hi = carve_2([P, NF, T], F16)
        s_lo = carve_2([P, NF, T], F16)
        sbd = carve_2([P, C], F32)
        carve_r = carver(work_region)
        carve_r([P, 2 * KC, T], F16)
        sig = carve_r([P, B * NT, E], F32)
        pick = carve_r([P, 2, B * NT, E], F32)
        key = carve_r([P, B * NT, E], F32)
        carve_r2 = carver(s_hi.rearrange("p f t -> p (f t)"))
        picked = carve_r2([P, B * NT, E], F16)
        best = carve_r2([P, 2, B * NT], F32)
        first = carve_r2([P, 2, B * NT], F32)
        pos = carve_r2([P, B * NT, E], F32)
        slot_f = carve_r2([P, 2, B * NT], F32)
        count = carve_r2([P, E], F32)
        count_i = carve_r2([P, E], I32)
        blocks = carve_r2([P, E], F32)
        last_block = carve_r2([P, 2, E], F32)
        before = carve_r2([1, BLOCKS, E], F32)
        block_f = carve_r2([1, BLOCKS], F32)
        sc_slot = sb("sc_slot", [P, 2, NT], U32)
        token_id = sb("token_id", [P, B * NT], F32)
        sc_token = sb("sc_token", [P, NT], F32)
        carve_3 = carver(work_region)
        xg = carve_3([P, 2, MT, 2 * C], F16)
        g_token = carve_3([P, 2, MT], U32)
        xgT = carve_3([P, 2 * KC, MB], F16)
        m_gelu = carve_3([P, 2, 2, MB], F32)
        m_hi = carve_3([P, NF, MB], F16)
        m_lo = carve_3([P, NF, MB], F16)
        m_y = carve_3([P, 2, MT, C], F32)
        bdn = carve_3([P, E, C], F32)
        slot_rows = carve_3([SLOTS // P, P], F32)
        carve_4 = carver(weights_region)
        c_res = carve_4([P, B * NT, C], F32)
        c_y = carve_4([P, B * NT, 2, C], F32)

        p1_done = sem("p1_done")
        route_step = sem("route_step")
        sig_ready = sem("sig_ready")
        picked_ready = sem("picked_ready")
        ranks_done = sem("ranks_done")
        routed = sem("routed")
        stage_in = [sem("stage_up_in"), sem("stage_down_in")]
        bias_in = sem("bias_in")
        w_hi_done = sem("w_hi_done")
        w_lo_done = sem("w_lo_done")
        xt_loaded = [sem("xt_loaded_0"), sem("xt_loaded_1")]
        r_loaded = [sem("r_loaded_0"), sem("r_loaded_1")]
        r_biased = sem("r_biased")
        sh_done = sem("sh_done")
        s_gelu_ready = sem("s_gelu_ready")
        s_hi_ready = sem("s_hi_ready")
        s_lo_ready = sem("s_lo_ready")
        s_out_done = sem("s_out_done")
        res_ready = sem("res_ready")
        res_stored = [sem("res_stored_0"), sem("res_stored_1")]
        slots_copied = sem("slots_copied")
        tokens_put = sem("tokens_put")
        slots_loaded = sem("slots_loaded")
        slotsT_done = sem("slotsT_done")
        tokens_ready = sem("tokens_ready")
        g_token_ready = sem("g_token_ready")
        gathered = [sem("gathered_0"), sem("gathered_1")]
        xgT_done = sem("xgT_done")
        xgT_ready = sem("xgT_ready")
        mh_done = sem("mh_done")
        m_gelu_ready = sem("m_gelu_ready")
        m_hi_ready = sem("m_hi_ready")
        m_lo_ready = sem("m_lo_ready")
        m_out_done = sem("m_out_done")
        y_out_ready = sem("y_out_ready")
        y_stored = [sem("y_stored_0"), sem("y_stored_1")]
        y_all = sem("y_all")
        c_res_in = sem("c_res_in")
        c_gathered = [sem(f"c_gathered_{g}") for g in range(B)]
        c_step = sem("c_step")
        c_done = sem("c_done")
        out_stored = sem("out_stored")

        consts_in = sem("consts_in")
        setup_done = sem("setup_done")
        x_loaded = sem("x_loaded")
        ctx_loaded = sem("ctx_loaded")
        dve_step = sem("dve_step")
        pool_step = sem("pool_step")
        var_ready = sem("var_ready")
        rstd_ready = sem("rstd_ready")
        ss_ready = sem("ss_ready")
        root_ready = sem("root_ready")
        xn1_ready = sem("xn1_ready")
        tr1_done = sem("tr1_done")
        xT_ready = sem("xT_ready")
        qkv_done = sem("qkv_done")
        sq_ready = sem("sq_ready")
        qk_copied = sem("qk_copied")
        v_ready = sem("v_ready")
        cos_ready = sem("cos_ready")
        rope_ready = sem("rope_ready")
        normed = sem("normed")
        aug_hi = sem("aug_hi")
        aug_ready = sem("aug_ready")
        augT_done = sem("augT_done")
        qt_ready = sem("qt_ready")
        kt_ready = sem("kt_ready")
        s1_done = sem("s1_done")
        s1_used = sem("s1_used")
        max_ready = sem("max_ready")
        maxT_done = sem("maxT_done")
        maxT_ready = sem("maxT_ready")
        max_rows = sem("max_rows")
        st_done = sem("st_done")
        exp_done = sem("exp_done")
        causal_done = sem("causal_done")
        pv_done = sem("pv_done")
        y_ready = sem("y_ready")
        den_ready = sem("den_ready")
        yn_ready = sem("yn_ready")
        proj_done = sem("proj_done")
        x1_ready = sem("x1_ready")
        xn2_ready = sem("xn2_ready")
        tr2_done = sem("tr2_done")
        x2T_hi = sem("x2T_hi")
        x2T_lo = sem("x2T_lo")
        ctx_hi_ready = sem("ctx_hi_ready")
        ctx_lo_ready = sem("ctx_lo_ready")
        h_done = sem("h_done")
        gelu_ready = sem("gelu_ready")
        act_ready = sem("act_ready")
        act_hi_ready = sem("act_hi_ready")
        act_lo_ready = sem("act_lo_ready")
        out_done = sem("out_done")
        x2_ready = sem("x2_ready")
        xn3_ready = sem("xn3_ready")
        xh_hi = sem("xh_hi")
        xh_lo = sem("xh_lo")
        tr3_done = sem("tr3_done")
        xT3_ready = sem("xT3_ready")
        gate_done = sem("gate_done")
        stored = sem("stored")
        passed = sem("passed")

        DVE_STEPS = NT * (3 * 2 + 2) + NG + 1
        CONSTS = 18 * 16
        SPLIT = 512
        PIECES = KC * F // SPLIT

        block = ctx.enter_context(nc.Block())

        @block.sync
        def _(sp):
            for dst, src in ((ident, A["ident"]), (identh, A["identh"]), (mask, A["mask"]),
                             (cos, A["cos"]), (sin, A["sin"]), (normw, A["normw"]),
                             (wqkv, A["wqkv"]), (gatew, A["gatew"]), (gateb, A["gateb"]),
                             (upper, A["upper"]), (eights, A["eights"]), (numbers, A["numbers"]),
                             (token_id, A["token_id"])):
                sp.dma_start(dst[:], src).then_inc(consts_in, 16)
            sp.wait_ge(setup_done, 2)
            sp.dma_start(token_dram.rearrange("(r c) o -> r (c o)", c=P),
                         QT[0:SLOTS // P, 0, 0:2 * P].bitcast(F32)).then_inc(consts_in, 16)
            for j in range(HG):
                sp.dma_start(wproj[32 * j:32 * j + D, :, :], A["wproj"][j]).then_inc(consts_in, 16)

            def load_x(b):
                sp.dma_start(x_in[:], A["x"][bass.ds(b, 1)].rearrange("o (i p) c -> p (o i) c", p=P)
                             ).then_inc(x_loaded, 16)

            def load_ctx(b):
                sp.dma_start(ctx_in[:, 0, :].rearrange("p (f c) -> p f c", f=NF),
                             A["ctx"][bass.ds(b, 1)].rearrange("o (f p) c -> p (o f) c", p=P)
                             ).then_inc(ctx_loaded, 16)
                sp.dma_start(ctx_in[:, 1, :].rearrange("p (k f) -> p k f", k=KC),
                             A["ctxT"][bass.ds(b, 1)].rearrange("o (k p) f -> p (o k) f", p=P)
                             ).then_inc(ctx_loaded, 16)

            def batch(b, last):
                for g in range(NG):
                    sp.wait_ge(maxT_ready, at(b, NG, g + 1))
                    for par in range(2):
                        sp.dma_start(QT[32 + 64 * par:33 + 64 * par, HG * g + par:HG * g + HG:2, :],
                                     mT[2 * par:2 * par + 2, g % 2, :]).then_inc(max_rows, 16)
                    if g == 1 and not last:
                        sp.wait_ge(ctx_hi_ready, at(b, 4, 4))
                        sp.wait_ge(ctx_lo_ready, at(b, 8, 8))
                        sp.sem_inc(passed, 1)
                        load_ctx(b + 1)
                if not last:
                    sp.wait_ge(x1_ready, at(b, NT, NT))
                    sp.sem_inc(passed, 1)
                    load_x(b + 1)
                sp.wait_ge(x2_ready, at(b, NT, NT))
                sp.sem_inc(passed, 1)
                sp.dma_start(x2_dram.rearrange("(b i p) c -> b p i c", p=P, i=NT)[bass.ds(b, 1)].rearrange("o p i c -> (o p) i c"),
                             x2[:]).then_inc(stored, 16)
                sp.wait_ge(xh_lo, at(b, NT, NT))
                sp.sem_inc(passed, 1)
                sp.dma_start(xh_dram.rearrange("(b i p) c -> b p i c", p=P, i=NT)[bass.ds(b, 1)].rearrange("o p i c -> (o p) i c"),
                             xh[:]).then_inc(stored, 16)
                sp.wait_ge(xT3_ready, at(b, NT, NT))
                sp.sem_inc(passed, 1)
                sp.dma_start(xt_dram[bass.ds(b, 1)].rearrange("o p n -> (o p) n"),
                             xT3[:].rearrange("p k t -> p (k t)")).then_inc(stored, 16)
                sp.wait_ge(stored, at(b, 48, 48))
                sp.sem_inc(passed, 1)

            load_x(0)
            load_ctx(0)
            with sp.Fori(0, B - 1) as b:
                batch(b, False)
            batch(B - 1, True)

            sp.wait_ge(p1_done, 1)
            for w, name in enumerate(("swu", "swd")):
                sp.dma_start(stage[:, w, :], A[name]).then_inc(stage_in[w], 16)
            sp.dma_start(bup[:], A["bup"]).then_inc(bias_in, 16)
            sp.dma_start(sbd[:], A["sbd"]).then_inc(bias_in, 16)

            def load_batch(b, u):
                sp.dma_start(xt_in[:, u].rearrange("p k t -> p (k t)"),
                             xt_dram[bass.ds(b, 1)].rearrange("o p n -> (o p) n")).then_inc(xt_loaded[u], 16)
                sp.dma_start(r_in[:, u], x2_dram.rearrange("(b i p) c -> b p i c", p=P, i=NT)[bass.ds(b, 1)].rearrange("o p i c -> (o p) i c")
                             ).then_inc(r_loaded[u], 16)

            def load_expert(e):
                for w, name in enumerate(("wu", "wd")):
                    sp.wait_ge(w_hi_done, at(e, 2 * PIECES, PIECES * (w + 1)))
                    sp.wait_ge(w_lo_done, at(e, 2 * PIECES, PIECES * (w + 1)))
                    sp.sem_inc(passed, 1)
                    sp.dma_start(stage[:, w, :], A[name][bass.ds(e, 1)].rearrange("o p n -> (o p) n")).then_inc(stage_in[w], 16)

            def store_batch(b, u):
                sp.wait_ge(res_ready, at(b, NT, NT))
                sp.sem_inc(passed, 1)
                sp.dma_start(res_dram.rearrange("(b i p) c -> b p i c", p=P, i=NT)[bass.ds(b, 1)].rearrange("o p i c -> (o p) i c"),
                             r_in[:, u]).then_inc(res_stored[u], 16)

            load_batch(0, 0)
            sp.wait_ge(routed, 1)
            load_batch(1, 1)
            with sp.Fori(0, B // 2 - 1) as it:
                for u in range(2):
                    load_expert(it * 2 + u)
                    store_batch(it * 2 + u, u)
                    sp.wait_ge(res_stored[u], at(it, 16, 16))
                    sp.sem_inc(passed, 1)
                    load_batch(it * 2 + u + 2, u)
            for b in (B - 2, B - 1):
                load_expert(b)
                store_batch(b, b % 2)
            for u in range(2):
                sp.wait_ge(res_stored[u], 16 * (B // 2))

            sp.wait_ge(tokens_put, 16 * 2 * B * NT)
            sp.wait_ge(w_lo_done, 2 * PIECES * (E + 1))
            sp.dma_start(slot_rows[:], token_dram.rearrange("(r c) o -> r (c o)", c=P)).then_inc(slots_loaded, 16)
            sp.dma_start(bdn[:], A["bdn"]).then_inc(slots_loaded, 16)

            def store_block(j, u):
                sp.wait_ge(y_out_ready, at(j, 1, 1))
                sp.sem_inc(passed, 1)
                sp.dma_start(y_dram.rearrange("(j i p) c -> j p i c", p=P, i=MT)[bass.ds(j, 1)].rearrange("o p i c -> (o p) i c"),
                             m_y[:, u]).then_inc(y_stored[u], 16)

            store_block(0, 0)
            with sp.Fori(0, BLOCKS // 2) as it:
                for u in range(2):
                    store_block(it * 2 + u + 1, 1 - u)
            sp.wait_ge(y_stored[0], 16 * (BLOCKS // 2 + 1))
            sp.wait_ge(y_stored[1], 16 * (BLOCKS // 2))
            sp.dma_start(c_res[:], res_dram.rearrange("(t p) c -> p t c", p=P)).then_inc(c_res_in, 16)
            sp.sem_inc(y_all, 1)
            for g in range(B):
                sp.wait_ge(c_done, g + 1)
                sp.dma_start(out.rearrange("b (i p) c -> b p i c", p=P)[g], c_res[:, NT * g:NT * g + NT, :]).then_inc(out_stored, 16)
            sp.wait_ge(out_stored, 16 * B)

        @block.vector
        def _(dve):
            nc.vector.memset(wproj[:], 0.0).then_inc(setup_done, 1)
            nc.vector.memset(QT[:], 0.0).then_inc(setup_done, 1)
            nc.vector.memset(aug[:], 0.0).then_inc(setup_done, 1)
            nc.vector.memset(vaug[:], 1.0).then_inc(setup_done, 1)
            dve.wait_ge(setup_done, 4)
            nc.vector.memset(aug[:, :, 1, :, 32:33], -1.0).then_inc(setup_done, 1)
            dve.wait_ge(consts_in, CONSTS)
            nc.vector.tensor_tensor(normw[:, 0, :], normw[:, 0, :], normw[:, 1, :], ALU.mult).then_inc(setup_done, 1)
            dve.wait_ge(setup_done, 6)
            nc.vector.tensor_scalar(normw[:, 1, :], normw[:, 0, :], float(D) ** -0.5, None, ALU.mult).then_inc(setup_done, 1)
            dve.wait_ge(setup_done, 7)
            for t in (cos, sin):
                nc.vector.tensor_tensor(t[:, :, 0, :], t[:, :, 0, :],
                                        normw[:, 1:2, :].to_broadcast([P, NT, D]), ALU.mult).then_inc(setup_done, 1)
            nc.vector.tensor_copy(gatew_hl[:, 0], gatew[:]).then_inc(setup_done, 1)
            dve.wait_ge(setup_done, 10)
            nc.vector.tensor_tensor(gatew_hl[:, 1], gatew[:], gatew_hl[:, 0], ALU.subtract).then_inc(setup_done, 1)
            nc.vector.memset(minus_half[:], -0.5).then_inc(setup_done, 1)
            dve.wait_ge(setup_done, 12)
            nc.vector.memset(plus_half[:], 0.5).then_inc(setup_done, 1)

            steps = [0]

            def batch(b):
                steps[0] = 0

                def link(ins):
                    steps[0] += 1
                    ins.then_inc(dve_step, 1)
                    dve.wait_ge(dve_step, at(b, DVE_STEPS, steps[0]))

                def moments(src, i):
                    link(nc.vector.bn_stats(stats[:, i, :], src[:, i, :]))
                    dve.sem_inc(passed, 1)
                    link(nc.vector.bn_aggr(mv[:, i, :], stats[:, i, :]))
                    nc.vector.tensor_scalar(mv[:, i, 1:2], mv[:, i, 1:2], 1e-5, None, ALU.add).then_inc(var_ready, 1)

                def normalize(src, i, norm, ready):
                    dve.wait_ge(rstd_ready, at(b, 3 * NT, norm * NT + i + 1))
                    nc.vector.tensor_scalar(xn[:, i, :], src[:, i, :], mv[:, i, 0:1], rstd[:, i:i + 1],
                                            ALU.subtract, ALU.mult).then_inc(ready, 1)

                dve.wait_ge(x_loaded, at(b, 16, 16))
                for i in range(NT + 1):
                    if i < NT:
                        moments(x_in, i)
                    if i >= 1:
                        normalize(x_in, i - 1, 0, xn1_ready)

                for i in range(NT + 3):
                    if i < NT:
                        u = i % 2
                        if i >= 2:
                            dve.wait_ge(rope_ready, at(b, NT, i - 1))
                        dve.wait_ge(qkv_done, at(b, NT, i + 1))
                        dve.wait_ge(qk_copied, at(b, NT, i + 1))
                        for w in range(2):
                            ins = nc.vector.tensor_tensor(
                                qk_cos[:, u, w * C:(w + 1) * C].rearrange("p (h d) -> p h d", d=D),
                                ps[:, u, w * C:(w + 1) * C].rearrange("p (h d) -> p h d", d=D),
                                cos[:, i, w:w + 1, :].to_broadcast([P, H, D]), ALU.mult)
                        ins.then_inc(cos_ready, 1)
                        dve.wait_ge(sq_ready, at(b, NT, i + 1))
                        nc.vector.tensor_reduce(qk_ss[:, u, :], qk_sq[:, u, :].rearrange("p (g d) -> p g d", d=D),
                                                AX_X, ALU.add).then_inc(ss_ready, 1)
                    if 1 <= i <= NT:
                        u = (i - 1) % 2
                        dve.wait_ge(rope_ready, at(b, NT, i))
                        v = qk_cos[:, u, :].rearrange("p (g d) -> p g d", d=D)
                        nc.vector.tensor_tensor(qk_sin[:, u, :].rearrange("p (g d) -> p g d", d=D), v,
                                                qk_ss[:, u, :].unsqueeze(2).to_broadcast([P, 2 * H, D]),
                                                ALU.mult).then_inc(normed, 1)
                    if i < NT:
                        u = i % 2
                        dve.wait_ge(root_ready, at(b, NT, i + 1))
                        link(nc.vector.tensor_scalar(qk_ss[:, u, :], qk_ss[:, u, :], float(D) ** -0.5, 1e-6, ALU.mult, ALU.add))
                        link(nc.vector.reciprocal(qk_ss[:, u, :], qk_ss[:, u, :]))
                    if 2 <= i <= NT + 1:
                        u = (i - 2) % 2
                        dve.wait_ge(aug_hi, at(b, NT, i - 1))
                        for w, c in ((0, 16), (1, 33)):
                            ins = nc.vector.tensor_tensor(
                                aug[:, u, w, :, c:c + D],
                                qk_sin[:, u, w * C:(w + 1) * C].rearrange("p (h d) -> p h d", d=D),
                                aug[:, u, w, :, 0:D], ALU.subtract)
                        ins.then_inc(aug_ready, 1)
                    if i >= 3:
                        j = i - 3
                        dve.wait_ge(augT_done, at(b, NT, j + 1))
                        t = half(4).rearrange("p (h t) -> p h t", t=P)
                        for par in range(2):
                            r = slice(64 * par, 64 * par + 64)
                            ins = nc.vector.tensor_copy(QT[r, par::2, j * P:(j + 1) * P], t[r])
                        ins.then_inc(qt_ready, 1)

                def maxima(h):
                    g, j = h // HG, h % HG
                    for r, tiles in enumerate(((3,), (2, 0), (1,))):
                        dve.wait_ge(s1_done, at(b, 3 * H, 3 * h + r + 1))
                        dve.sem_inc(passed, 1)
                        for i in tiles:
                            w = (i + 1) * P
                            c = 384 if i == 0 else 0
                            ins = nc.vector.tensor_tensor_reduce(
                                ps[:, 3 + r, c:c + w], ps[:, 3 + r, c:c + w], mask[:, T - w:T], 1.0, -BIG,
                                ALU.add, ALU.max, mx[:, i, h:h + 1])
                        ins.then_inc(s1_used, 1)
                    if j == HG - 1:
                        dve.wait_ge(s1_used, at(b, 3 * H, 3 * h + 3))
                        for par in range(2):
                            ins = nc.vector.tensor_copy(mx16[:, g, :, 2 * par:2 * par + 2],
                                                        mx[:, :, HG * g + par:HG * g + HG:2])
                        ins.then_inc(max_ready, 1)

                def maxT(g):
                    dve.wait_ge(maxT_done, at(b, NG, g + 1))
                    nc.vector.tensor_copy(mT[:, g % 2, :], half(7)[0:HG, 0:T]).then_inc(maxT_ready, 1)

                def denominators(g):
                    dve.wait_ge(y_ready, at(b, NG, g + 1))
                    dve.sem_inc(passed, 1)
                    link(nc.vector.stream_shuffle(den[:, g % 2, :], y_sb[:, g % 2, :], [D] * 32))
                    nc.vector.reciprocal(den[:, g % 2, :], den[:, g % 2, :]).then_inc(den_ready, 1)

                for h in range(H):
                    maxima(h)
                    if h % HG == 1 and h > HG:
                        maxT(h // HG - 1)
                    if h % HG == 3 and h // HG >= 3:
                        denominators(h // HG - 3)
                maxT(NG - 1)
                for g in range(1, NG):
                    denominators(g)

                for i in range(NT + 2):
                    if i < NT:
                        dve.wait_ge(proj_done, at(b, NT, i + 1))
                        nc.vector.tensor_tensor(x1[:, i, :], x_in[:, i, :], ps[:, 3 + i % 2, 0:C], ALU.add).then_inc(x1_ready, 1)
                        dve.wait_ge(x1_ready, at(b, NT, i + 1))
                        moments(x1, i)
                    if 1 <= i <= NT:
                        normalize(x1, i - 1, 1, xn2_ready)
                    if i >= 2:
                        j = i - 2
                        dve.wait_ge(x2T_hi, at(b, NT, j + 1))
                        nc.vector.tensor_tensor(xT_lo[:, :, j * P:(j + 1) * P],
                                                ps[:, 6 + j % 2, 0:C].rearrange("p (k t) -> p k t", k=KC),
                                                xT_hi[:, :, j * P:(j + 1) * P], ALU.subtract).then_inc(x2T_lo, 1)

                for f in range(NF):
                    dve.wait_ge(gelu_ready, at(b, NF, f + 1))
                    if f >= 2:
                        dve.wait_ge(act_lo_ready, at(b, NF, f - 1))
                    nc.vector.tensor_tensor(act[:, f % 2, :], ps[:, f % 3, :], gelu[:, f % 2, :], ALU.mult).then_inc(act_ready, 1)

                for i in range(NT + 2):
                    if i < NT:
                        dve.wait_ge(out_done, at(b, NT, i + 1))
                        nc.vector.tensor_tensor(x2[:, i, :], x1[:, i, :], ps[:, 3 + i % 2, 0:C], ALU.add).then_inc(x2_ready, 1)
                        dve.wait_ge(x2_ready, at(b, NT, i + 1))
                        moments(x2, i)
                    if 1 <= i <= NT:
                        normalize(x2, i - 1, 2, xn3_ready)
                    if i >= 2:
                        j = i - 2
                        dve.wait_ge(xh_hi, at(b, NT, j + 1))
                        nc.vector.tensor_tensor(xh[:, j, C:2 * C], xn[:, j, :], xh[:, j, 0:C], ALU.subtract).then_inc(xh_lo, 1)
                dve.wait_ge(gate_done, at(b, NT, NT))
                link(nc.vector.tensor_tensor(
                    logits[:, bass.ds(b * NT, NT), :], ps[:, 5, 0:NT * E].rearrange("p (i e) -> p i e", e=E),
                    gateb[:].unsqueeze(1).to_broadcast([P, NT, E]), ALU.add))

            with dve.Fori(0, B) as b:
                batch(b)
            assert steps[0] == DVE_STEPS
            nc.vector.memset(onesh[:], 1.0).then_inc(p1_done, 1)

            routes = [0]

            def step(ins):
                routes[0] += 1
                ins.then_inc(route_step, 1)
                dve.wait_ge(route_step, routes[0])

            every = [P, B * NT, E]
            dve.wait_ge(sig_ready, 1)
            for n in range(2):
                step(nc.vector.tensor_reduce(best[:, n, :], sig[:], AX_X, ALU.max))
                step(nc.vector.tensor_tensor(key[:], sig[:], best[:, n, :].unsqueeze(2).to_broadcast(every), ALU.is_equal))
                step(nc.vector.tensor_tensor(key[:], key[:], eights[:].unsqueeze(1).to_broadcast(every), ALU.mult))
                step(nc.vector.tensor_reduce(first[:, n, :], key[:], AX_X, ALU.max))
                step(nc.vector.tensor_tensor(pick[:, n], eights[:].unsqueeze(1).to_broadcast(every),
                                             first[:, n, :].unsqueeze(2).to_broadcast(every), ALU.is_equal))
                if n == 0:
                    step(nc.vector.scalar_tensor_tensor(sig[:].rearrange("p t e -> p (t e)"), pick[:, 0].rearrange("p t e -> p (t e)"), -4.0,
                                                        sig[:].rearrange("p t e -> p (t e)"), ALU.mult, ALU.add))
            nc.vector.tensor_tensor(picked[:], pick[:, 0], pick[:, 1], ALU.add).then_inc(picked_ready, 1)
            step(nc.vector.tensor_tensor(first[:, 0, :], best[:, 0, :], best[:, 1, :], ALU.add))
            step(nc.vector.tensor_scalar(first[:, 0, :], first[:, 0, :], 1e-6, None, ALU.add))
            step(nc.vector.reciprocal(first[:, 0, :], first[:, 0, :]))
            step(nc.vector.tensor_tensor(share[:], best[:], first[:, 0:1, :].to_broadcast([P, 2, B * NT]), ALU.mult))
            dve.wait_ge(ranks_done, 1)
            step(nc.vector.tensor_scalar(count[:], ps[:, 6, 0:E], float(MB - 1), None, ALU.add))
            step(nc.vector.tensor_copy(count_i[:], count[:]))
            step(nc.vector.tensor_scalar(count_i[:], count_i[:], MB.bit_length() - 1, None, ALU.arith_shift_right))
            step(nc.vector.tensor_copy(blocks[:], count_i[:]))
            step(nc.vector.tensor_copy(last_block[:, 0, :], blocks[:]))
            a = 0
            for d in (1, 2, 4):
                step(nc.vector.tensor_copy(last_block[:, 1 - a, 0:d], last_block[:, a, 0:d]))
                step(nc.vector.tensor_tensor(last_block[:, 1 - a, d:E], last_block[:, a, d:E], last_block[:, a, 0:E - d], ALU.add))
                a = 1 - a
            step(nc.vector.tensor_tensor(before[:], numbers[:].unsqueeze(2).to_broadcast([1, BLOCKS, E]),
                                         last_block[0:1, a:a + 1, :].to_broadcast([1, BLOCKS, E]), ALU.is_ge))
            step(nc.vector.tensor_reduce(block_f[:], before[:], AX_X, ALU.add))
            step(nc.vector.tensor_scalar(block_f[:], block_f[:], float(E - 1), None, ALU.min))
            step(nc.vector.tensor_copy(block_expert[:], block_f[:]))
            step(nc.vector.tensor_tensor(blocks[:], last_block[:, a, :], blocks[:], ALU.subtract))
            step(nc.vector.tensor_scalar(blocks[:], blocks[:], float(MB), None, ALU.mult))
            step(nc.vector.tensor_tensor(pos[:], ps[:, 5, 0:B * NT * E].rearrange("p (t e) -> p t e", e=E),
                                         blocks[:].unsqueeze(1).to_broadcast(every), ALU.add))
            for n in range(2):
                step(nc.vector.tensor_tensor(key[:], pick[:, n], pos[:], ALU.mult))
                step(nc.vector.tensor_reduce(slot_f[:, n, :], key[:], AX_X, ALU.add))
            nc.vector.tensor_copy(slot_u[:], slot_f[:]).then_inc(routed, 1)
            dve.wait_ge(bias_in, 32)
            step(nc.vector.tensor_scalar(sbd[:], sbd[:], 0.1, None, ALU.mult))
            nc.vector.memset(sc_token[:, 0:1], 0.0).then_inc(routed, 1)

            with dve.Fori(0, B // 2) as it:
                for u in range(2):
                    b = it * 2 + u
                    for f in range(NF):
                        dve.wait_ge(s_gelu_ready, at(b, NF, f + 1))
                        nc.vector.tensor_copy(s_hi[:, f, :], s_gelu[:, f % 2, :]).then_inc(s_hi_ready, 1)
                        dve.wait_ge(s_hi_ready, at(b, NF, f + 1))
                        nc.vector.tensor_tensor(s_lo[:, f, :], s_gelu[:, f % 2, :], s_hi[:, f, :], ALU.subtract).then_inc(s_lo_ready, 1)
                    dve.wait_ge(r_biased, at(b, 1, 1))
                    for i in range(NT):
                        dve.wait_ge(s_out_done, at(b, NT, i + 1))
                        nc.vector.scalar_tensor_tensor(r_in[:, u, i, :], ps[:, 3 + i % 2, 0:C], 0.1, r_in[:, u, i, :],
                                                       ALU.mult, ALU.add).then_inc(res_ready, 1)

            dve.wait_ge(slotsT_done, 1)
            nc.vector.tensor_copy(tokens_u[:], ps[:, 6, 0:SLOTS // P]).then_inc(tokens_ready, 1)

            def block_in(j):
                dve.wait_ge(xgT_done, at(j, 1, 1))
                nc.vector.tensor_copy(xgT[:].rearrange("p k t -> p (k t)"), half(7)).then_inc(xgT_ready, 1)

            def block_split(j):
                for q in range(NF // 2):
                    dve.wait_ge(m_gelu_ready, at(j, NF, 2 * q + 2))
                    g = m_gelu[:, q % 2]
                    nc.vector.tensor_copy(m_hi[:, 2 * q:2 * q + 2, :], g).then_inc(m_hi_ready, 1)
                    dve.wait_ge(m_hi_ready, at(j, NF // 2, q + 1))
                    nc.vector.tensor_tensor(m_lo[:, 2 * q:2 * q + 2, :], g, m_hi[:, 2 * q:2 * q + 2, :], ALU.subtract).then_inc(m_lo_ready, 1)

            def block_out(j, u, stored):
                e = nc.vector.value_load(block_expert[0:1, bass.ds(j, 1)], min_val=0, max_val=E - 1)
                dve.wait_ge(m_out_done, at(j, 1, 1))
                if stored is not None:
                    dve.wait_ge(y_stored[u], 16 * stored)
                nc.vector.tensor_tensor(m_y[:, u], ps[:, 4 + u, :].rearrange("p (i c) -> p i c", i=MT),
                                        bdn[:, bass.ds(e, 1), :].to_broadcast([P, MT, C]), ALU.add).then_inc(y_out_ready, 1)

            dve.wait_ge(slots_loaded, 32)
            block_in(0)
            block_split(0)

            def pair(it, first):
                for u in range(2):
                    j = it * 2 + u + 1
                    block_in(j)
                    block_out(j - 1, u, None if first else it)
                    block_split(j)

            pair(0, True)
            with dve.Fori(1, BLOCKS // 2) as it:
                pair(it, False)
            block_out(BLOCKS - 1, 0, BLOCKS // 2)

            dve.wait_ge(c_res_in, 16)
            for g in range(B):
                dve.wait_ge(c_gathered[g], 16 * 2 * NT)
                for n in range(2):
                    for i in range(NT):
                        t = NT * g + i
                        if n == 1:
                            dve.wait_ge(c_step, t + 1)
                        ins = nc.vector.scalar_tensor_tensor(c_res[:, t, :], c_y[:, t, n, :], share[:, n, t:t + 1], c_res[:, t, :],
                                                             ALU.mult, ALU.add)
                        if n == 0:
                            ins.then_inc(c_step, 1)
                ins.then_inc(c_done, 1)

        @block.scalar
        def _(sc):
            sc.wait_ge(setup_done, 13)
            with sc.Fori(0, B) as b:
                for i in range(NT):
                    sc.wait_ge(tr1_done, at(b, NT, i + 1))
                    nc.scalar.copy(xT[:, :, i * P:(i + 1) * P],
                                   ps[:, 6 + i % 2, 0:C].rearrange("p (k t) -> p k t", k=KC)).then_inc(xT_ready, 1)
                for i in range(NT + 3):
                    if i < NT:
                        u = i % 2
                        if i >= 2:
                            sc.wait_ge(rope_ready, at(b, NT, i - 1))
                            sc.wait_ge(normed, at(b, NT, i - 1))
                        sc.wait_ge(qkv_done, at(b, NT, i + 1))
                        nc.scalar.activation(qk_sq[:, u, :], ps[:, u, :], ACT.Square).then_inc(sq_ready, 1)
                        nc.scalar.copy(qk_sb[:, u, :], ps[:, u, :]).then_inc(qk_copied, 1)
                        nc.scalar.copy(vaug[:, i, :, 0:D],
                                       ps[:, 2 + u, 0:C].rearrange("p (h d) -> p h d", d=D)).then_inc(v_ready, 1)
                    if 1 <= i <= NT:
                        j, u = i - 1, (i - 1) % 2
                        sc.wait_ge(normed, at(b, NT, j + 1))
                        if j >= 2:
                            sc.wait_ge(augT_done, at(b, NT, j - 1))
                        for w, step in ((0, 33), (1, 16)):
                            src = qk_sin[:, u, w * C:(w + 1) * C].rearrange("p (h d) -> p h d", d=D)
                            for c in range(2):
                                ins = nc.scalar.copy(aug[:, u, w, :, step * c:step * c + D], src)
                        ins.then_inc(aug_hi, 1)
                    if i >= 3:
                        j = i - 3
                        sc.wait_ge(augT_done, at(b, NT, j + 1))
                        nc.scalar.copy(KT[:, :, j * P:(j + 1) * P],
                                       half(5).rearrange("p (h t) -> p h t", t=P)).then_inc(kt_ready, 1)
                sc.wait_ge(ctx_loaded, at(b, 32, 32))
                for w in range(2):
                    for c in range(2):
                        nc.scalar.copy(ctx_hi[:, w, c * 1024:(c + 1) * 1024],
                                       ctx_in[:, w, c * 1024:(c + 1) * 1024]).then_inc(ctx_hi_ready, 1)

                def evacuate(g):
                    if g >= 2:
                        sc.wait_ge(yn_ready, at(b, NG, g - 1))
                    sc.wait_ge(pv_done, at(b, NG, g + 1))
                    nc.scalar.copy(y_sb[:, g % 2, :], ps[:, 6, :]).then_inc(y_ready, 1)

                for h in range(H):
                    g, j = h // HG, h % HG
                    if g >= 2 and j == 0:
                        sc.wait_ge(pv_done, at(b, NG, g - 1))
                    sc.wait_ge(st_done, at(b, H, h + 1))
                    nc.scalar.activation(probs[:, g % 2, j, :],
                                         ps[:, 0:3, :].rearrange("p b c -> p (b c)")[:, 0:PT_W],
                                         ACT.Exp).then_inc(exp_done, 1)
                    if g >= 1 and j == 2:
                        evacuate(g - 1)
                evacuate(NG - 1)

                for i in range(NT):
                    sc.wait_ge(tr2_done, at(b, NT, i + 1))
                    nc.scalar.copy(xT_hi[:, :, i * P:(i + 1) * P],
                                   ps[:, 6 + i % 2, 0:C].rearrange("p (k t) -> p k t", k=KC)).then_inc(x2T_hi, 1)
                for f in range(NF + 1):
                    if f < NF:
                        sc.wait_ge(h_done, at(b, NF, f + 1))
                        if f >= 2:
                            sc.wait_ge(act_ready, at(b, NF, f - 1))
                        nc.scalar.activation(gelu[:, f % 2, :], ps[:, f % 3, :], ACT.Gelu).then_inc(gelu_ready, 1)
                    if f >= 1:
                        sc.wait_ge(act_ready, at(b, NF, f))
                        nc.scalar.copy(act_hi[:, f - 1, :], act[:, (f - 1) % 2, :]).then_inc(act_hi_ready, 1)
                for i in range(NT + 1):
                    if i < NT:
                        sc.wait_ge(xn3_ready, at(b, NT, i + 1))
                        nc.scalar.copy(xh[:, i, 0:C], xn[:, i, :]).then_inc(xh_hi, 1)
                    if i >= 1:
                        j = i - 1
                        sc.wait_ge(tr3_done, at(b, NT, j + 1))
                        nc.scalar.copy(xT3[:, :, j * P:(j + 1) * P],
                                       half(6 + j % 2)[:, 0:T].rearrange("p (k t) -> p k t", k=2 * KC)
                                       ).then_inc(xT3_ready, 1)

            sc.wait_ge(p1_done, 1)
            nc.scalar.activation(sig[:], logits[:], ACT.Sigmoid).then_inc(sig_ready, 1)
            for w in range(2):
                sc.wait_ge(stage_in[w], 16)
                for c in range(PIECES):
                    q = slice(c * SPLIT, (c + 1) * SPLIT)
                    nc.scalar.copy(w_shared[:, w, 0, q], stage[:, w, q]).then_inc(w_hi_done, 1)
            sc.wait_ge(bias_in, 32)
            with sc.Fori(0, B // 2) as it:
                for u in range(2):
                    b = it * 2 + u
                    for f in range(NF):
                        sc.wait_ge(sh_done, at(b, NF, f + 1))
                        if f >= 2:
                            sc.wait_ge(s_lo_ready, at(b, NF, f - 1))
                        nc.scalar.activation(s_gelu[:, f % 2, :], ps[:, f % 3, :], ACT.Gelu,
                                             bias=bup[:, E, f:f + 1]).then_inc(s_gelu_ready, 1)
                        w, c = f // PIECES, f % PIECES
                        if c == 0:
                            sc.wait_ge(stage_in[w], at(b, 16, 32))
                        q = slice(c * SPLIT, (c + 1) * SPLIT)
                        nc.scalar.copy(weights[:, w, 0, bass.ds(b, 1), q], stage[:, w:w + 1, q]).then_inc(w_hi_done, 1)

            def block_gelu(j):
                e = nc.scalar.value_load(block_expert[0:1, bass.ds(j, 1)], min_val=0, max_val=E - 1)
                for f in range(NF):
                    q = f // 2
                    if f % 2 == 0:
                        sc.wait_ge(mh_done, at(j, NF // 2, q + 1))
                    if q >= 2 and f % 2 == 0:
                        sc.wait_ge(m_lo_ready, at(j, NF // 2, q - 1))
                    sc.sem_inc(passed, 1)
                    nc.scalar.activation(m_gelu[:, q % 2, f % 2, :], ps[:, q, (f % 2) * MB:(f % 2 + 1) * MB], ACT.Gelu,
                                         bias=bup[:, bass.ds(e, 1), f:f + 1].rearrange("p o n -> p (o n)")).then_inc(m_gelu_ready, 1)

            block_gelu(0)
            with sc.Fori(0, BLOCKS // 2) as it:
                for u in range(2):
                    block_gelu(it * 2 + u + 1)

        @block.gpsimd
        def _(pool):
            pool.wait_ge(setup_done, 13)
            with pool.Fori(0, B) as b:
                def inverse_root(norm, i):
                    pool.wait_ge(var_ready, at(b, 3 * NT, norm * NT + i + 1))
                    nc.gpsimd.tensor_tensor(rstd[:, i:i + 1], mv[:, i, 1:2], minus_half[:], ALU.pow).then_inc(rstd_ready, 1)

                for i in range(NT):
                    inverse_root(0, i)
                for i in range(NT):
                    u = i % 2
                    pool.wait_ge(ss_ready, at(b, NT, i + 1))
                    nc.gpsimd.tensor_tensor(qk_ss[:, u, :], qk_ss[:, u, :], plus_half[:].to_broadcast([P, 2 * H]),
                                            ALU.pow).then_inc(root_ready, 1)
                    pool.wait_ge(qk_copied, at(b, NT, i + 1))
                    if i >= 2:
                        pool.wait_ge(aug_ready, at(b, NT, i - 1))
                    a = qk_sb[:, u, :].rearrange("p (w h d) -> p w h d", w=2, d=D)
                    o = qk_sin[:, u, :].rearrange("p (w h d) -> p w h d", w=2, d=D)
                    for w in range(2):
                        for z in range(2):
                            to, fr = slice(8 * z, 8 * z + 8), slice(8 - 8 * z, 16 - 8 * z)
                            ins = nc.gpsimd.tensor_tensor(o[:, w, :, to], a[:, w, :, fr],
                                                          sin[:, i, w:w + 1, to].to_broadcast([P, H, 8]), ALU.mult)
                    ins.then_inc(pool_step, 1)
                    pool.wait_ge(pool_step, at(b, NT, i + 1))
                    pool.wait_ge(cos_ready, at(b, NT, i + 1))
                    nc.gpsimd.tensor_tensor(qk_cos[:, u, :], qk_cos[:, u, :], qk_sin[:, u, :], ALU.add).then_inc(rope_ready, 1)
                for w in range(2):
                    for c in range(4):
                        pool.wait_ge(ctx_hi_ready, at(b, 4, 2 * w + c // 2 + 1))
                        q = slice(c * 512, (c + 1) * 512)
                        nc.gpsimd.tensor_tensor(ctx_lo[:, w, q], ctx_in[:, w, q], ctx_hi[:, w, q],
                                                ALU.subtract).then_inc(ctx_lo_ready, 1)

                def divide(g):
                    pool.wait_ge(den_ready, at(b, NG, g + 1))
                    nc.gpsimd.tensor_tensor(yn[:, g, :], y_sb[:, g % 2, :], den[:, g % 2, :],
                                            ALU.mult).then_inc(yn_ready, 1)

                for h in range(H):
                    g, j = h // HG, h % HG
                    pool.wait_ge(exp_done, at(b, H, h + 1))
                    pool.sem_inc(passed, 1)
                    v = probs[:, g % 2, j, :]
                    for c in (0, 384, 512, 1024):
                        ins = nc.gpsimd.affine_select(out=v[:, c:c + P], in_=v[:, c:c + P], compare_op=ALU.is_ge,
                                                      fill=0.0, base=0, pattern=[[1, P]], channel_multiplier=-1)
                    ins.then_inc(causal_done, 1)
                    if g >= 2 and j == 1:
                        divide(g - 2)
                divide(NG - 2)
                divide(NG - 1)
                for i in range(NT):
                    inverse_root(1, i)
                for f in range(NF):
                    pool.wait_ge(act_hi_ready, at(b, NF, f + 1))
                    nc.gpsimd.tensor_tensor(act_lo[:, f, :], act[:, f % 2, :], act_hi[:, f, :],
                                            ALU.subtract).then_inc(act_lo_ready, 1)
                for i in range(NT):
                    inverse_root(2, i)

            for w in range(2):
                for c in range(PIECES):
                    pool.wait_ge(w_hi_done, PIECES * w + c + 1)
                    q = slice(c * SPLIT, (c + 1) * SPLIT)
                    nc.gpsimd.tensor_tensor(w_shared[:, w, 1, q], stage[:, w, q], w_shared[:, w, 0, q], ALU.subtract).then_inc(w_lo_done, 1)
            pool.wait_ge(routed, 2)
            with pool.Fori(0, B // 2) as it:
                for u in range(2):
                    b = it * 2 + u
                    pool.wait_ge(r_loaded[u], at(it, 16, 16))
                    nc.gpsimd.tensor_tensor(r_in[:, u], r_in[:, u], sbd[:].unsqueeze(1).to_broadcast([P, NT, C]), ALU.add).then_inc(r_biased, 1)
                    nc.gpsimd.tensor_copy(sc_slot[:], slot_u[:, :, bass.ds(b * NT, NT)]).then_inc(slots_copied, 1)
                    nc.gpsimd.tensor_copy(sc_token[:], token_id[:, bass.ds(b * NT, NT)]).then_inc(slots_copied, 1)
                    pool.wait_ge(slots_copied, at(b, 2, 2))
                    pool.sem_inc(passed, 1)
                    for f in range(NF):
                        i, n = f // 2, f % 2
                        nc.gpsimd.indirect_dma_start(token_dram, bass.IndirectOffsetOnAxis(sc_slot[:, n, i:i + 1], 0),
                                                     sc_token[:, i:i + 1], None).then_inc(tokens_put, 16)
                        w, c = f // PIECES, f % PIECES
                        pool.wait_ge(w_hi_done, at(b, 2 * PIECES, 2 * PIECES + f + 1))
                        q = slice(c * SPLIT, (c + 1) * SPLIT)
                        nc.gpsimd.tensor_tensor(weights[:, w, 1, bass.ds(b, 1), q], stage[:, w:w + 1, q],
                                                weights[:, w, 0, bass.ds(b, 1), q], ALU.subtract).then_inc(w_lo_done, 1)
                    pool.wait_ge(tokens_put, at(b, 16 * 2 * NT, 16 * 2 * NT))
                    pool.sem_inc(passed, 1)

            pool.wait_ge(tokens_ready, 1)

            def gather(j, u):
                nc.gpsimd.tensor_copy(g_token[:, u, :], tokens_u[:, bass.ds(j * MT, MT)]).then_inc(g_token_ready, 1)
                pool.wait_ge(g_token_ready, at(j, 1, 1))
                pool.sem_inc(passed, 1)
                for i in range(MT):
                    nc.gpsimd.indirect_dma_start(xg[:, u, i, :], None, xh_dram,
                                                 bass.IndirectOffsetOnAxis(g_token[:, u, i:i + 1], 0)).then_inc(gathered[u], 16)

            gather(0, 0)
            gather(1, 1)
            with pool.Fori(0, BLOCKS // 2 - 1) as it:
                for u in range(2):
                    pool.wait_ge(xgT_done, at(it, 2, u + 1))
                    gather(it * 2 + u + 2, u)
            pool.wait_ge(xgT_done, BLOCKS - 2)
            gather(BLOCKS - 1, 0)

            pool.wait_ge(y_all, 1)
            for g in range(B):
                for i in range(NT):
                    t = NT * g + i
                    for n in range(2):
                        nc.gpsimd.indirect_dma_start(c_y[:, t, n, :], None, y_dram,
                                                     bass.IndirectOffsetOnAxis(slot_u[:, n, t:t + 1], 0)).then_inc(c_gathered[g], 16)

        @block.tensor
        def _(pe):
            pe.wait_ge(setup_done, 13)
            pe.wait_ge(consts_in, CONSTS)
            with pe.Fori(0, B) as b:
                def transposes(i):
                    for k in range(KC):
                        ins = nc.tensor.transpose(ps[:, 6 + i % 2, k * P:(k + 1) * P], xn[:, i, k * P:(k + 1) * P], ident[:])
                    return ins

                for i in range(NT):
                    pe.wait_ge(xn1_ready, at(b, NT, i + 1))
                    if i >= 2:
                        pe.wait_ge(xT_ready, at(b, NT, i - 1))
                    transposes(i).then_inc(tr1_done, 1)

                def qkv(i):
                    u = i % 2
                    pe.wait_ge(xT_ready, at(b, NT, i + 1))
                    if i >= 2:
                        pe.wait_ge(cos_ready, at(b, NT, i - 1))
                        pe.wait_ge(v_ready, at(b, NT, i - 1))
                    for k in range(KC):
                        nc.tensor.matmul(ps[:, u, :], xT[:, k, i * P:(i + 1) * P], wqkv[:, k, 0:2 * C],
                                         start=(k == 0), stop=(k == KC - 1))
                    for k in range(KC):
                        ins = nc.tensor.matmul(ps[:, 2 + u, 0:C], xT[:, k, i * P:(i + 1) * P], wqkv[:, k, 2 * C:3 * C],
                                               start=(k == 0), stop=(k == KC - 1))
                    ins.then_inc(qkv_done, 1)

                def augT(i):
                    pe.wait_ge(aug_ready, at(b, NT, i + 1))
                    if i >= 1:
                        pe.wait_ge(qt_ready, at(b, NT, i))
                        pe.wait_ge(kt_ready, at(b, NT, i))
                    for w in range(2):
                        for q in range(H // 2):
                            ins = nc.tensor.transpose(half(4 + w)[:, q * P:(q + 1) * P],
                                                      aug[:, i % 2, w, 2 * q:2 * q + 2, :].rearrange("p h c -> p (h c)"), identh[:])
                    ins.then_inc(augT_done, 1)

                for i in range(NT):
                    qkv(i)
                    if i >= 2:
                        augT(i - 2)
                augT(NT - 2)
                augT(NT - 1)
                pe.wait_ge(qt_ready, at(b, NT, NT))
                pe.wait_ge(kt_ready, at(b, NT, NT))
                pe.wait_ge(v_ready, at(b, NT, NT))

                def scores(h):
                    for r, tiles in enumerate(((3,), (2, 0), (1,))):
                        if h >= 1:
                            pe.wait_ge(s1_used, at(b, 3 * H, 3 * (h - 1) + r + 1))
                        for i in tiles:
                            w = (i + 1) * P
                            c = 384 if i == 0 else 0
                            ins = nc.tensor.matmul(ps[:, 3 + r, c:c + w], QT[:, h, i * P:(i + 1) * P], KT[:, h // 2, 0:w],
                                                   start=True, stop=True)
                        ins.then_inc(s1_done, 1)

                def maxT(g):
                    pe.wait_ge(max_ready, at(b, NG, g + 1))
                    if g >= 1:
                        pe.wait_ge(maxT_ready, at(b, NG, g))
                    for i in range(NT):
                        ins = nc.tensor.transpose(half(7)[0:HG, i * P:(i + 1) * P], mx16[:, g, i, :], identh[:])
                    ins.then_inc(maxT_done, 1)

                def scoresT(h):
                    if h % HG == 0:
                        pe.wait_ge(max_rows, at(b, 32 * NG, 32 * (h // HG + 1)))
                    if h >= 1:
                        pe.wait_ge(exp_done, at(b, H, h))
                    flat = ps[:, 0:3, :].rearrange("p b c -> p (b c)")
                    for s in (0, 1, 2, 3):
                        c, w = PT_AT[s], T - s * P
                        ins = nc.tensor.matmul(flat[:, c:c + w], KT[:, h // 2, s * P:(s + 1) * P], QT[:, h, s * P:T],
                                               start=True, stop=True)
                    ins.then_inc(st_done, 1)

                def values(g):
                    pe.wait_ge(causal_done, at(b, H, HG * (g + 1)))
                    if g >= 1:
                        pe.wait_ge(y_ready, at(b, NG, g))
                    for s in range(NT):
                        c, w = PT_AT[s], T - s * P
                        for j in range(HG):
                            ins = nc.tensor.matmul(ps[32 * j:32 * j + 32, 6, s * P:T], vaug[:, s, HG * g + j, :],
                                                   probs[:, g % 2, j, c:c + w], start=(s == 0), stop=(s == NT - 1))
                    ins.then_inc(pv_done, 1)

                for h in range(2 * HG):
                    scores(h)
                    if h == HG + 1:
                        maxT(0)
                for g in range(NG):
                    for j in range(HG):
                        scoresT(HG * g + j)
                        if g + 2 < NG:
                            scores(HG * (g + 2) + j)
                        if j == 1 and g + 1 < NG:
                            maxT(g + 1)
                        if j == 1 and g >= 1:
                            values(g - 1)
                values(NG - 1)

                def project(i):
                    if i == 0:
                        pe.wait_ge(yn_ready, at(b, NG, NG))
                    if i >= 2:
                        pe.wait_ge(x1_ready, at(b, NT, i - 1))
                    for g in range(NG):
                        ins = nc.tensor.matmul(ps[:, 3 + i % 2, 0:C], yn[:, g, i * P:(i + 1) * P], wproj[:, g, :],
                                               start=(g == 0), stop=(g == NG - 1))
                    ins.then_inc(proj_done, 1)

                def tr2(i):
                    pe.wait_ge(xn2_ready, at(b, NT, i + 1))
                    if i >= 2:
                        pe.wait_ge(x2T_lo, at(b, NT, i - 1))
                    transposes(i).then_inc(tr2_done, 1)

                for i in range(NT):
                    project(i)
                    if i >= 1:
                        tr2(i - 1)
                tr2(NT - 1)
                pe.wait_ge(x2T_lo, at(b, NT, NT))
                pe.wait_ge(ctx_lo_ready, at(b, 8, 8))
                for f in range(NF):
                    if f >= 3:
                        pe.wait_ge(act_ready, at(b, NF, f - 2))
                    n = 0
                    for k in range(KC):
                        for w, a in ((ctx_cols[0], xT_hi), (ctx_cols[0], xT_lo), (ctx_cols[1], xT_hi)):
                            ins = nc.tensor.matmul(ps[:, f % 3, :], w[:, k, f * P:(f + 1) * P], a[:, k, :],
                                                   start=(n == 0), stop=(n == 5))
                            n += 1
                    ins.then_inc(h_done, 1)

                def xout(i):
                    if i >= 2:
                        pe.wait_ge(x2_ready, at(b, NT, i - 1))
                    for f in range(NF):
                        if i == 0:
                            pe.wait_ge(act_lo_ready, at(b, NF, f + 1))
                        for n, (a, w) in enumerate(((act_hi, 0), (act_hi, 1), (act_lo, 0))):
                            ins = nc.tensor.matmul(ps[:, 3 + i % 2, 0:C], a[:, f, i * P:(i + 1) * P], ctx_rows[w][:, f, :],
                                                   start=(f == 0 and n == 0), stop=(f == NF - 1 and n == 2))
                    ins.then_inc(out_done, 1)

                def tr3(i):
                    pe.wait_ge(xh_lo, at(b, NT, i + 1))
                    if i >= 2:
                        pe.wait_ge(xT3_ready, at(b, NT, i - 1))
                    for k in range(2 * KC):
                        ins = nc.tensor.transpose(half(6 + i % 2)[:, k * P:(k + 1) * P], xh[:, i, k * P:(k + 1) * P], identh[:])
                    ins.then_inc(tr3_done, 1)

                def gate(i):
                    pe.wait_ge(xT3_ready, at(b, NT, i + 1))
                    n = 0
                    for k in range(KC):
                        for a, w in ((k, 0), (k, 1), (KC + k, 0)):
                            ins = nc.tensor.matmul(ps[:, 5, i * E:(i + 1) * E], xT3[:, a, i * P:(i + 1) * P], gatew_hl[:, w, k, :],
                                                   start=(n == 0), stop=(n == 5))
                            n += 1
                    ins.then_inc(gate_done, 1)

                for i in range(NT):
                    xout(i)
                    if i >= 2:
                        tr3(i - 2)
                tr3(NT - 2)
                tr3(NT - 1)
                for i in range(NT):
                    gate(i)

            pe.wait_ge(picked_ready, 1)
            flat = picked[:].rearrange("p t e -> p (t e)")
            nc.tensor.matmul(ps[:, 5, 0:B * NT * E], upper[:], flat, start=True, stop=False, skip_group_check=True)
            for d in range(1, B * NT):
                nc.tensor.matmul(ps[:, 5, d * E:B * NT * E], onesh[:], flat[:, 0:(B * NT - d) * E],
                                 start=False, stop=(d == B * NT - 1), skip_group_check=True)
            for t in range(B * NT):
                ins = nc.tensor.matmul(ps[:, 6, 0:E], onesh[:], flat[:, t * E:(t + 1) * E], start=(t == 0), stop=(t == B * NT - 1))
            ins.then_inc(ranks_done, 1)

            up = [w_shared[:, 0, n].rearrange("p (k f) -> p k f", k=KC) for n in range(2)]
            down = [w_shared[:, 1, n].rearrange("p (f c) -> p f c", f=NF) for n in range(2)]
            pe.wait_ge(w_lo_done, 2 * PIECES)
            with pe.Fori(0, B // 2) as it:
                for u in range(2):
                    b = it * 2 + u
                    pe.wait_ge(xt_loaded[u], at(it, 16, 16))
                    for f in range(NF):
                        if f >= 3:
                            pe.wait_ge(s_gelu_ready, at(b, NF, f - 2))
                        n = 0
                        for k in range(KC):
                            for w, a in ((0, k), (0, KC + k), (1, k)):
                                ins = nc.tensor.matmul(ps[:, f % 3, :], up[w][:, k, f * P:(f + 1) * P], xt_in[:, u, a, :],
                                                       start=(n == 0), stop=(n == 5))
                                n += 1
                        ins.then_inc(sh_done, 1)
                    for i in range(NT):
                        if i >= 2:
                            pe.wait_ge(res_ready, at(b, NT, i - 1))
                        for f in range(NF):
                            if i == 0:
                                pe.wait_ge(s_lo_ready, at(b, NF, f + 1))
                            for n, (a, w) in enumerate(((s_hi, 0), (s_hi, 1), (s_lo, 0))):
                                ins = nc.tensor.matmul(ps[:, 3 + i % 2, 0:C], a[:, f, i * P:(i + 1) * P], down[w][:, f, :],
                                                       start=(f == 0 and n == 0), stop=(f == NF - 1 and n == 2))
                        ins.then_inc(s_out_done, 1)

            pe.wait_ge(slots_loaded, 32)
            nc.tensor.transpose(ps[:, 6, 0:SLOTS // P], slot_rows[:], ident[0:SLOTS // P, 0:SLOTS // P]).then_inc(slotsT_done, 1)
            pe.wait_ge(w_lo_done, 2 * PIECES * (E + 1))

            def block_T(j, u, count):
                pe.wait_ge(gathered[u], count)
                pe.sem_inc(passed, 1)
                for k in range(2 * KC):
                    for i in range(MT):
                        ins = nc.tensor.transpose(half(7)[:, (k * MT + i) * P:(k * MT + i + 1) * P],
                                                  xg[:, u, i, k * P:(k + 1) * P], identh[:])
                ins.then_inc(xgT_done, 1)

            def block_up(j, e):
                pe.wait_ge(xgT_ready, at(j, 1, 1))
                pe.sem_inc(passed, 1)
                for f in range(NF):
                    n = 0
                    for k in range(KC):
                        for w, a in ((0, k), (0, KC + k), (1, k)):
                            c = k * F + f * P
                            ins = nc.tensor.matmul(ps[:, f // 2, (f % 2) * MB:(f % 2 + 1) * MB],
                                                   weights[:, 0, w, bass.ds(e, 1), c:c + P].rearrange("p o n -> p (o n)"),
                                                   xgT[:, a, :], start=(n == 0), stop=(n == 5), skip_group_check=True)
                            n += 1
                    if f % 2 == 1:
                        ins.then_inc(mh_done, 1)

            def block_down(j, e, u):
                for i in range(MT):
                    for f in range(NF):
                        if i == 0 and f % 2 == 0:
                            pe.wait_ge(m_lo_ready, at(j, NF // 2, f // 2 + 1))
                            pe.sem_inc(passed, 1)
                        for n, (a, w) in enumerate(((m_hi, 0), (m_hi, 1), (m_lo, 0))):
                            ins = nc.tensor.matmul(ps[:, 4 + u, i * C:(i + 1) * C], a[:, f, i * P:(i + 1) * P],
                                                   weights[:, 1, w, bass.ds(e, 1), f * C:(f + 1) * C].rearrange("p o n -> p (o n)"),
                                                   start=(f == 0 and n == 0), stop=(f == NF - 1 and n == 2), skip_group_check=True)
                ins.then_inc(m_out_done, 1)

            def expert(j):
                return nc.tensor.value_load(block_expert[0:1, bass.ds(j, 1)], min_val=0, max_val=E - 1)

            block_T(0, 0, 32)
            block_up(0, expert(0))
            with pe.Fori(0, BLOCKS // 2) as it:
                for u in range(2):
                    j = it * 2 + u + 1
                    block_T(j, 1 - u, at(it, 32, 32 + 32 * u))
                    block_down(j - 1, expert(j - 1), u)
                    block_up(j, expert(j))
            block_down(BLOCKS - 1, expert(BLOCKS - 1), 0)


def layouts(inp):
    f = np.float32
    a = {k: np.asarray(v) for k, v in inp.items()}
    w = a["L0_attn_W_kqv"]
    w_qkv = np.concatenate([w[C:2 * C], w[0:C], w[2 * C:3 * C]], 0)
    pos = np.arange(T, dtype=f)
    inv = (1.0 / np.float32(10000.0) ** (np.arange(0, D, 2, dtype=f) / np.float32(D))).astype(f)
    fr = (pos[:, None] * inv[None, :]).astype(f)
    cos = np.cos(np.concatenate([fr, fr], -1)).astype(f).reshape(NT, P, 1, D).transpose(1, 0, 2, 3)
    sin = np.sin(np.concatenate([-fr, fr], -1)).astype(f).reshape(NT, P, 1, D).transpose(1, 0, 2, 3)
    tri = np.where(np.arange(P)[None, :] > np.arange(P)[:, None], -BIG / 10, 0.0).astype(f)
    return {
        "x": a["x"],
        "ctx": a["ctx_1024"],
        "ctxT": a["ctx_1024"].transpose(0, 2, 1),
        "wqkv": w_qkv.T.reshape(KC, P, 3 * C).transpose(1, 0, 2),
        "wproj": a["L0_attn_W_proj"].T.reshape(NG, HG, D, C).transpose(1, 2, 0, 3),
        "normw": np.broadcast_to(np.stack([a["L0_attn_q_norm_w"], a["L0_attn_k_norm_w"]]), (P, 2, D)),
        "cos": np.broadcast_to(cos, (P, NT, 2, D)),
        "sin": np.broadcast_to(sin, (P, NT, 2, D)),
        "mask": np.concatenate([np.zeros((P, T - P), f), tri], 1),
        "ident": np.eye(P, dtype=f),
        "identh": np.eye(P, dtype=np.float16),
        "gatew": a["L0_ffn_gate_w"].T.reshape(KC, P, E).transpose(1, 0, 2),
        "gateb": np.broadcast_to(a["L0_ffn_gate_bias"], (P, E)),
        "upper": np.triu(np.ones((P, P), np.float16), 1),
        "eights": np.broadcast_to(np.arange(E, 0, -1, dtype=f), (P, E)),
        "numbers": np.arange(BLOCKS, dtype=f)[None],
        "token_id": np.arange(N, dtype=f).reshape(B * NT, P).T,
        "swu": a["L0_ffn_sWu"].T.reshape(KC, P, F).transpose(1, 0, 2).reshape(P, KC * F),
        "swd": a["L0_ffn_sWd"].T.reshape(NF, P, C).transpose(1, 0, 2).reshape(P, NF * C),
        "wu": a["L0_ffn_Wu"].transpose(0, 2, 1).reshape(E, KC, P, F).transpose(0, 2, 1, 3).reshape(E, P, KC * F),
        "wd": a["L0_ffn_Wd"].transpose(0, 2, 1).reshape(E, NF, P, C).transpose(0, 2, 1, 3).reshape(E, P, NF * C),
        "bup": np.concatenate([a["L0_ffn_bu"], a["L0_ffn_sbu"][None]], 0).reshape(E + 1, NF, P).transpose(2, 0, 1),
        "sbd": np.broadcast_to(a["L0_ffn_sbd"], (P, C)),
        "bdn": np.broadcast_to(a["L0_ffn_bd"], (P, E, C)),
    }


def kernel(**inputs):
    import numpy as _np
    import concourse.bacc as _bacc
    from concourse import mybir as _mybir
    from concourse.bass_utils import run_bass_kernel_spmd as _run

    nc = _bacc.Bacc("TRN2", target_bir_lowering=False, num_devices=1)
    arrays, args = {}, {}
    for name, a in layouts(inputs).items():
        a = _np.ascontiguousarray(a)
        arrays[f"in_{name}"] = a
        args[name] = nc.dram_tensor(f"in_{name}", a.shape, _mybir.dt.from_np(a.dtype), kind="ExternalInput").ap()
    out = nc.dram_tensor("out_0", (B, T, C), _mybir.dt.float32, kind="ExternalOutput").ap()
    decoder_kernel(nc, args, out)
    r = _run(nc, [arrays], core_ids=[0])
    return r.results[0]["out_0"]
```

```python
from contextlib import ExitStack

import numpy as np

import concourse.bass as bass
from concourse import mybir

F32 = mybir.dt.float32
F16 = mybir.dt.float16
I32 = mybir.dt.int32
U32 = mybir.dt.uint32
ALU = mybir.AluOpType
ACT = mybir.ActivationFunctionType
AX_X = mybir.AxisListType.X

P = 128
B, T, C = 8, 512, 256
H, D = 16, 16
NT = T // P
KC = C // P
S = 1024
NF = S // P
HG = 4
NG = H // HG
E = 8
F = 1024
N = B * T
BIG = 3.0e38

PT_AT = {1: 0, 3: 384, 0: 512, 2: 1024}
PT_W = 1280
WORK = 57 * 1024
MB = 256
MT = MB // P
BLOCKS = (2 * N + E * (MB - 1)) // MB
UNROLL = 2
assert BLOCKS % UNROLL == 1
SLOTS = BLOCKS * MB


def at(b, per, count):
    return b * per + count


def decoder_kernel(nc, A, out):
    ctx = ExitStack()
    with ctx:
        def sb(name, shape, dt):
            return ctx.enter_context(nc.sbuf_tensor(name, shape, dt))

        def sem(name):
            return ctx.enter_context(nc.semaphore(name))

        def dram(name, shape, dt):
            return nc.dram_tensor(name, shape, dt, kind="Internal").ap()

        x2_dram = dram("x2_dram", (N, C), F32)
        xh_dram = dram("xh_dram", (N, 2 * C), F16)
        xt_dram = dram("xt_dram", (B, P, 2 * KC * T), F16)
        slot_dram = dram("slot_dram", (SLOTS, 2), F32)
        res_dram = dram("res_dram", (N + MB, C), F32)

        ps = ctx.enter_context(nc.psum_tensor("ps", [P, 8, 512], F32))

        def half(bank, n=1):
            return ps[:, bank:bank + n, :].rearrange("p b c -> p (b c)").bitcast(F16)

        weights_region = sb("weights_region", [P, 2 * 2 * E * KC * F], F16)
        work_region = sb("work_region", [P, WORK // 2], F16)

        def carver(region):
            used = [0]

            def carve(shape, dt):
                size = 4 if dt != F16 else 2
                n = int(np.prod(shape[1:])) * size // 2
                piece = region[0:shape[0], used[0]:used[0] + n]
                used[0] += n
                assert used[0] <= region.shape[1], used
                if dt != F16:
                    piece = piece.bitcast(dt)
                dims = " ".join(f"d{i}" for i in range(len(shape) - 1))
                sizes = {f"d{i}": n for i, n in enumerate(shape[1:])}
                return piece.rearrange(f"p ({dims}) -> p {dims}", **sizes) if len(shape) > 2 else piece

            return carve

        ident = sb("ident", [P, P], F32)
        identh = sb("identh", [P, P], F16)
        normw = sb("normw", [P, 2, D], F32)
        gatew = sb("gatew", [P, KC, E], F32)
        gatew_hl = sb("gatew_hl", [P, 2, KC, E], F16)
        gateb = sb("gateb", [P, E], F32)
        carve_w, carve_k = carver(weights_region), carver(work_region)
        probs = carve_w([P, 2, HG, PT_W], F32)
        wqkv_in = probs[:, 0].rearrange("p h c -> p (h c)")[:, 0:KC * 3 * C].rearrange("p (k c) -> p k c", k=KC)
        carve_o = carver(weights_region)
        mask = carve_k([P, T], F32)
        cos = carve_k([P, NT, 2, D], F32)
        sin = carve_k([P, NT, 2, D], F32)
        wqkv = carve_k([P, 2, KC, 3 * C], F16)
        wproj = carve_k([P, NG // 2, C], F32)
        x_in = carve_k([P, NT, C], F32)
        xn = carve_k([P, NT, C], F32)
        xn1 = carve_k([P, NT, C], F32)
        res = carve_k([P, NT, C], F32)
        minus_half = sb("minus_half", [P, 1], F32)
        stats = sb("stats", [P, NT, 6], F32)
        mv = sb("mv", [P, NT, 2], F32)
        rstd = sb("rstd", [P, NT], F32)
        xT = carve_k([P, 2, KC, T], F16)
        qk_sb = carve_w([P, 2, 2 * C], F32)
        qk_sq = carve_w([P, 2, 2 * C], F32)
        qk_cos = carve_w([P, 2, 2 * C], F32)
        qk_sin = carve_w([P, 2, 2 * C], F32)
        qk_ss = sb("qk_ss", [P, 2, 2 * H], F32)
        aug = carve_k([P, 2, 2, H, 64], F16)
        QT = carve_w([P, H, T], F16)
        KT = carve_w([P, H // 2, T], F16)
        vaug = carve_w([P, NT, H, 32], F32)
        mx = carve_k([P, NT, H], F32)
        mx16 = carve_k([P, NG, NT, HG], F16)
        mT = carve_k([HG, 2, T], F16)
        yn = carve_w([P, NG // 2, T], F32)
        yT = carve_w([P, T], F32)
        pairT = carve_w([P, T], F32)
        ctx_in = carve_w([P, 2, 2048], F32)
        ctx_hi = carve_w([P, 2, 2048], F16)
        ctx_lo = carve_w([P, 2, 2048], F16)
        xT_hi = carve_k([P, KC, T], F16)
        xT_lo = carve_k([P, KC, T], F16)
        gelu = carve_o([P, 2, T], F32)
        act = carve_o([P, 4, T], F32)
        act_hi = carve_o([P, NF, T], F16)
        act_lo = carve_o([P, NF, T], F16)
        xh = carve_k([P, NT, 2 * C], F16)
        xT3 = carve_k([P, 2 * KC, T], F16)
        logits = sb("logits", [P, B * NT, E], F32)

        ctx_rows = [t[:, 0, :].rearrange("p (f c) -> p f c", f=NF) for t in (ctx_hi, ctx_lo)]
        ctx_cols = [t[:, 1, :].rearrange("p (k f) -> p k f", k=KC) for t in (ctx_hi, ctx_lo)]

        weights = weights_region[:].rearrange("p (w h e n) -> p w h e n", w=2, h=2, e=E)
        w_shared = sb("w_shared", [P, 2, 2, KC * F], F16)
        slot_u = sb("slot_u", [P, 2, B * NT], U32)
        share = sb("share", [P, 2, B * NT], F32)
        bup = sb("bup", [P, E + 1, F // P], F32)
        block_expert = sb("block_expert", [1, BLOCKS], I32)
        tokens_u = sb("tokens_u", [P, 2, SLOTS // P], U32)
        slot_share = sb("slot_share", [P, SLOTS // P], F32)
        upper = sb("upper", [P, P], F16)
        onesh = sb("onesh", [P, P], F16)
        eights = sb("eights", [P, E], F32)
        numbers = sb("numbers", [1, BLOCKS], F32)
        carve_2 = carver(work_region)
        xt_in = carve_2([P, 2, 2 * KC, T], F16)
        stage = carve_2([P, 2, KC * F], F32)
        r_in = carve_2([P, 2, NT, C], F32)
        s_gelu = carve_2([P, 2, T], F32)
        s_hi = carve_2([P, NF, T], F16)
        s_lo = carve_2([P, NF, T], F16)
        sbd = carve_2([P, C], F32)
        carve_r = carver(r_in[:, 1].rearrange("p i c -> p (i c)").bitcast(F16))
        sig = carve_r([P, B * NT, E], F32)
        pick = carve_r([P, 2, B * NT, E], F32)
        key = carve_r([P, B * NT, E], F32)
        behind = carve_2([P, 2 * MT * 2 * C], F16)
        xg = behind.rearrange("p (u i c) -> p u i c", u=2, i=MT)
        carve_r2 = carver(behind)
        picked = carve_r2([P, B * NT, E], F16)
        best = carve_r2([P, 2, B * NT], F32)
        first = carve_r2([P, 2, B * NT], F32)
        pos = carve_r2([P, B * NT, E], F32)
        slot_f = carve_r2([P, 2, B * NT], F32)
        count = carve_r2([P, E], F32)
        count_i = carve_r2([P, E], I32)
        blocks = carve_r2([P, E], F32)
        last_block = carve_r2([P, 2, E], F32)
        before = carve_r2([1, BLOCKS, E], F32)
        block_f = carve_r2([1, BLOCKS], F32)
        sc_slot = sb("sc_slot", [P, 2, NT], U32)
        slot_rows = sb("slot_rows", [SLOTS // P, P, 2], F32)
        g_token = sb("g_token", [P, 2, MT], U32)
        g_dest = sb("g_dest", [P, MT], U32)
        g_share = sb("g_share", [P, MT], F32)
        token_id = sb("token_id", [P, B * NT], F32)
        sc_token = sb("sc_token", [P, NT, 2, 2], F32)
        carve_3 = carver(work_region)
        xgT = carve_3([P, 2 * KC, MB], F16)
        m_gelu = carve_3([P, 2, 2, MB], F32)
        m_hi = carve_3([P, NF, MB], F16)
        m_lo = carve_3([P, NF, MB], F16)
        m_y = carve_3([P, 2, MT, C], F32)
        bdn = carve_3([P, E, C], F32)

        p1_done = sem("p1_done")
        route_step = sem("route_step")
        sig_ready = sem("sig_ready")
        picked_ready = sem("picked_ready")
        ranks_done = sem("ranks_done")
        routed = sem("routed")
        stage_in = [sem("stage_up_in"), sem("stage_down_in")]
        bias_in = sem("bias_in")
        bias_scaled = sem("bias_scaled")
        w_hi_done = sem("w_hi_done")
        w_lo_done = sem("w_lo_done")
        w_lo_down_done = sem("w_lo_down_done")
        xt_loaded = [sem("xt_loaded_0"), sem("xt_loaded_1")]
        r_loaded = [sem("r_loaded_0"), sem("r_loaded_1")]
        r_biased = sem("r_biased")
        sh_done = sem("sh_done")
        s_gelu_ready = sem("s_gelu_ready")
        s_hi_ready = sem("s_hi_ready")
        s_lo_ready = sem("s_lo_ready")
        s_out_done = sem("s_out_done")
        res_ready = sem("res_ready")
        res_stored = [sem("res_stored_0"), sem("res_stored_1")]
        slots_copied = sem("slots_copied")
        tokens_put = sem("tokens_put")
        slots_loaded = sem("slots_loaded")
        bdn_loaded = sem("bdn_loaded")
        slotsT_done = sem("slotsT_done")
        tokens_ready = sem("tokens_ready")
        g_token_ready = sem("g_token_ready")
        gathered = [sem("gathered_0"), sem("gathered_1")]
        xgT_done = sem("xgT_done")
        xgT_ready = sem("xgT_ready")
        mh_done = sem("mh_done")
        m_gelu_ready = sem("m_gelu_ready")
        m_hi_ready = sem("m_hi_ready")
        m_lo_ready = sem("m_lo_ready")
        m_out_done = sem("m_out_done")
        y_out_ready = sem("y_out_ready")
        g_share_ready = sem("g_share_ready")
        g_dest_ready = sem("g_dest_ready")
        y_sum_ready = sem("y_sum_ready")
        added = sem("added")
        out_stored = sem("out_stored")

        consts_in = sem("consts_in")
        first_in = sem("first_in")
        tables_in = sem("tables_in")
        setup_done = sem("setup_done")
        cleared = sem("cleared")
        cleared_queries = sem("cleared_queries")
        x_loaded = sem("x_loaded")
        res_loaded = sem("res_loaded")
        logits_ready = sem("logits_ready")
        ctx_loaded = sem("ctx_loaded")
        front_step = sem("front_step")
        norm_step = sem("norm_step")
        divide_step = sem("divide_step")
        var1_ready = sem("var1_ready")
        rstd1_ready = sem("rstd1_ready")
        pool_step = sem("pool_step")
        var_ready = sem("var_ready")
        rstd_ready = sem("rstd_ready")
        ss_ready = sem("ss_ready")
        root_ready = sem("root_ready")
        xn1_ready = sem("xn1_ready")
        tr1_done = sem("tr1_done")
        xT_ready = sem("xT_ready")
        xT_low_ready = sem("xT_low_ready")
        wqkv_high = sem("wqkv_high")
        wqkv_low = sem("wqkv_low")
        qkv_done = sem("qkv_done")
        sq_ready = sem("sq_ready")
        qk_copied = sem("qk_copied")
        v_ready = sem("v_ready")
        cos_ready = sem("cos_ready")
        rope_ready = sem("rope_ready")
        normed = sem("normed")
        aug_hi = sem("aug_hi")
        aug_ready = sem("aug_ready")
        augT_done = sem("augT_done")
        qt_ready = sem("qt_ready")
        kt_ready = sem("kt_ready")
        s1_done = sem("s1_done")
        s1_used = sem("s1_used")
        max_ready = sem("max_ready")
        maxT_done = sem("maxT_done")
        maxT_ready = sem("maxT_ready")
        max_rows = sem("max_rows")
        st_done = sem("st_done")
        exp_done = sem("exp_done")
        causal_done = sem("causal_done")
        pv_done = sem("pv_done")
        y_taken = sem("y_taken")
        yn_ready = sem("yn_ready")
        proj_done = sem("proj_done")
        x1_ready = sem("x1_ready")
        xn2_ready = sem("xn2_ready")
        tr2_done = sem("tr2_done")
        x2T_hi = sem("x2T_hi")
        x2T_lo = sem("x2T_lo")
        ctx_hi_ready = sem("ctx_hi_ready")
        ctx_lo_ready = sem("ctx_lo_ready")
        h_done = sem("h_done")
        gelu_ready = sem("gelu_ready")
        act_ready = sem("act_ready")
        act_hi_ready = sem("act_hi_ready")
        act_lo_ready = sem("act_lo_ready")
        out_done = sem("out_done")
        x2_ready = sem("x2_ready")
        xn3_ready = sem("xn3_ready")
        xh_hi = sem("xh_hi")
        xh_lo = sem("xh_lo")
        tr3_done = sem("tr3_done")
        xT3_ready = sem("xT3_ready")
        gate_done = sem("gate_done")
        x2_stored = sem("x2_stored")
        xh_stored = sem("xh_stored")
        passed = sem("passed")

        CONSTS = 11 * 16
        AHEAD = 7
        HIDDEN_BANK = (0, 3, 4)
        OUT_BANK = (1, 2, 0, 1)
        EARLY = 2
        CUT = 12
        PARTS = (((1, 3), 0, 512), ((0, 2), 512, PT_W))
        SPLIT = 512
        PIECES = KC * F // SPLIT

        block = ctx.enter_context(nc.Block())

        @block.sync
        def _(sp):
            def load_x(b):
                sp.dma_start(x_in[:], A["x"][bass.ds(b, 1)].rearrange("o (i p) c -> p (o i) c", p=P)
                             ).then_inc(x_loaded, 16)

            def load_ctx(b):
                sp.dma_start(ctx_in[:, 0, :].rearrange("p (f c) -> p f c", f=NF),
                             A["ctx"][bass.ds(b, 1)].rearrange("o (f p) c -> p (o f) c", p=P)
                             ).then_inc(ctx_loaded, 16)
                sp.dma_start(ctx_in[:, 1, :].rearrange("p (k f) -> p k f", k=KC),
                             A["ctxT"][bass.ds(b, 1)].rearrange("o (k p) f -> p (o k) f", p=P)
                             ).then_inc(ctx_loaded, 16)

            def rows(t, b):
                return t.rearrange("(b i p) c -> b p i c", p=P, i=NT)[bass.ds(b, 1)].rearrange("o p i c -> (o p) i c")

            def load_res(b):
                sp.dma_start(res[:], A["x"][bass.ds(b, 1)].rearrange("o (i p) c -> p (o i) c", p=P)
                             ).then_inc(res_loaded, 16)

            def load_xt(b, u):
                sp.dma_start(xt_in[:, u].rearrange("p k t -> p (k t)"),
                             xt_dram[bass.ds(b, 1)].rearrange("o p n -> (o p) n")).then_inc(xt_loaded[u], 16)

            def store_norm3(b):
                sp.wait_ge(xh_lo, at(b, NT, NT))
                sp.sem_inc(passed, 1)
                sp.dma_start(rows(xh_dram, b), xh[:]).then_inc(xh_stored, 16)
                sp.wait_ge(xT3_ready, at(b, NT, NT))
                sp.sem_inc(passed, 1)
                sp.dma_start(xt_dram[bass.ds(b, 1)].rearrange("o p n -> (o p) n"),
                             xT3[:].rearrange("p k t -> p (k t)")).then_inc(xh_stored, 16)
                sp.wait_ge(x2_stored, at(b, 16, 16))
                sp.sem_inc(passed, 1)

            def batch(b, first, last):
                for g in range(NG):
                    sp.wait_ge(maxT_ready, at(b, NG, g + 1))
                    for par in range(2):
                        sp.dma_start(QT[32 + 64 * par:33 + 64 * par, HG * g + par:HG * g + HG:2, :],
                                     mT[2 * par:2 * par + 2, g % 2, :]).then_inc(max_rows, 16)
                    if g == 0 and not first:
                        store_norm3(b - 1)
                        load_res(b)
                    if g == 1 and not first:
                        sp.wait_ge(xh_stored, at(b, 32, 0))
                        sp.sem_inc(passed, 1)
                    if g == 0 and not last:
                        sp.wait_ge(xn1_ready, at(b, NT, NT))
                        sp.sem_inc(passed, 1)
                        load_x(b + 1)
                    if g == 1 and not last:
                        sp.wait_ge(ctx_hi_ready, at(b, 4, 4))
                        sp.wait_ge(ctx_lo_ready, at(b, 8, 8))
                        sp.sem_inc(passed, 1)
                        load_ctx(b + 1)
                    if g == 1 and last:
                        sp.wait_ge(ctx_hi_ready, at(b, 4, 4))
                        sp.wait_ge(ctx_lo_ready, at(b, 8, 8))
                        for w, name in enumerate(("swu", "swd")):
                            sp.dma_start(ctx_in[:, w, :], A[name]).then_inc(stage_in[w], 16)
                if last:
                    sp.wait_ge(x1_ready, at(b, NT, NT))
                    load_xt(0, 0)
                sp.wait_ge(x2_ready, at(b, NT, NT))
                sp.sem_inc(passed, 1)
                sp.dma_start(rows(x2_dram, b), res[:]).then_inc(x2_stored, 16)

            load_x(0)
            for dst, src in ((ident[:], A["ident"]), (wqkv_in, A["wqkv"])):
                sp.dma_start(dst, src).then_inc(first_in, 16)
            for dst, src in ((cos, A["cos"]), (sin, A["sin"]), (normw, A["normw"])):
                sp.dma_start(dst[:], src).then_inc(tables_in, 16)
            for dst, src in ((identh, A["identh"]), (mask, A["mask"]),
                             (gatew, A["gatew"]), (gateb, A["gateb"]),
                             (upper, A["upper"]), (eights, A["eights"]), (numbers, A["numbers"]),
                             (token_id, A["token_id"]), (wproj, A["wproj"])):
                sp.dma_start(dst[:], src).then_inc(consts_in, 16)
            load_ctx(0)
            load_res(0)
            sp.dma_start(slot_dram, A["padding"]).then_inc(consts_in, 16)
            sp.dma_start(res_dram[N:N + MB, :], A["x"][0, 0:MB, :]).then_inc(consts_in, 16)
            batch(0, True, False)
            with sp.Fori(1, B - 1) as b:
                batch(b, False, False)
            batch(B - 1, False, True)
            store_norm3(B - 1)
            sp.wait_ge(xh_stored, 32 * B)

            sp.wait_ge(p1_done, 1)
            sp.dma_start(bup[:], A["bup"]).then_inc(bias_in, 16)
            sp.dma_start(sbd[:], A["sbd"]).then_inc(bias_in, 16)

            def load_r(b, u):
                sp.dma_start(r_in[:, u], x2_dram.rearrange("(b i p) c -> b p i c", p=P, i=NT)[bass.ds(b, 1)].rearrange("o p i c -> (o p) i c")
                             ).then_inc(r_loaded[u], 16)

            def load_expert(e, first=None):
                for w, name in enumerate(("wu", "wd")):
                    sp.wait_ge(w_hi_done, at(e, 2 * PIECES, PIECES * (w + 1)))
                    if w == 0:
                        sp.wait_ge(w_lo_done, at(e, PIECES, 2 * PIECES))
                    elif first is None:
                        sp.wait_ge(w_lo_down_done, at(e, PIECES, 0))
                    sp.sem_inc(passed, 1)
                    sp.dma_start(stage[:, w, :], A[name][bass.ds(e, 1)].rearrange("o p n -> (o p) n")).then_inc(stage_in[w], 16)

            def store_batch(b, u):
                sp.wait_ge(res_ready, at(b, NT, NT))
                sp.sem_inc(passed, 1)
                sp.dma_start(res_dram[0:N, :].rearrange("(b i p) c -> b p i c", p=P, i=NT)[bass.ds(b, 1)].rearrange("o p i c -> (o p) i c"),
                             r_in[:, u]).then_inc(res_stored[u], 16)

            def turn(b, u, next_expert):
                load_expert(next_expert)
                store_batch(b, u)

            def refill(b, u):
                load_xt(b, u)
                load_r(b, u)

            load_r(0, 0)
            load_expert(0, True)
            load_xt(1, 1)
            load_expert(1)
            sp.wait_ge(routed, 1)
            load_r(1, 1)
            store_batch(0, 0)
            sp.wait_ge(res_stored[0], 16)
            refill(2, 0)
            turn(1, 1, 2)
            sp.wait_ge(res_stored[1], 16)
            refill(3, 1)
            with sp.Fori(1, B // 2 - 1) as it:
                for u in range(2):
                    turn(it * 2 + u, u, it * 2 + u + 1)
                    sp.wait_ge(res_stored[u], at(it, 16, 16))
                    sp.sem_inc(passed, 1)
                    refill(it * 2 + u + 2, u)
            load_expert(B - 1)
            store_batch(B - 2, 0)
            sp.wait_ge(tokens_put, 16 * 2 * B * NT)
            sp.dma_start(slot_rows[:], slot_dram.rearrange("(r c) o -> r (c o)", c=P)).then_inc(slots_loaded, 16)
            store_batch(B - 1, 1)
            for u in range(2):
                sp.wait_ge(res_stored[u], 16 * (B // 2))
            sp.wait_ge(w_lo_done, PIECES * (E + 2))
            sp.wait_ge(w_lo_down_done, PIECES * E)
            sp.dma_start(bdn[:], A["bdn"]).then_inc(bdn_loaded, 16)
            sp.wait_ge(added, 16 * MT * BLOCKS)
            sp.dma_start(out.rearrange("b t c -> (b t) c"), res_dram[0:N, :]).then_inc(out_stored, 16)
            sp.wait_ge(out_stored, 16)

        @block.vector
        def _(dve):

            steps = {"front": 0, "norm": 0, "divide": 0}

            def link(ins, kind, signal, b, per):
                steps[kind] += 1
                ins.then_inc(signal, 1)
                dve.wait_ge(signal, at(b, per, steps[kind]))

            FRONT, NORM, DIVIDE = NT * 4, NT * 4, NG * 2

            def moments(src, i, kind, signal, b, per, ready):
                link(nc.vector.bn_stats(stats[:, i, :], src[:, i, :]), kind, signal, b, per)
                dve.sem_inc(passed, 1)
                link(nc.vector.bn_aggr(mv[:, i, :], stats[:, i, :]), kind, signal, b, per)
                nc.vector.tensor_scalar(mv[:, i, 1:2], mv[:, i, 1:2], 1e-5, None, ALU.add).then_inc(ready, 1)

            def normalize(dst, src, i, ready):
                nc.vector.tensor_scalar(dst[:, i, :], src[:, i, :], mv[:, i, 0:1], rstd[:, i:i + 1],
                                        ALU.subtract, ALU.mult).then_inc(ready, 1)

            def norm1_begin(b):
                steps["front"] = 0
                dve.wait_ge(x_loaded, at(b, 16, 16))
                for i in range(2):
                    moments(x_in, i, "front", front_step, b, FRONT, var1_ready)

            def norm1_end(b):
                for i in range(NT):
                    dve.wait_ge(rstd1_ready, at(b, NT, i + 1))
                    normalize(xn1, x_in, i, xn1_ready)
                    if i + 2 < NT:
                        moments(x_in, i + 2, "front", front_step, b, FRONT, var1_ready)

            def norm1_low(b, i):
                dve.wait_ge(xT_ready, at(b, NT, i + 1))
                nc.vector.tensor_tensor(xT[:, 1, :, i * P:(i + 1) * P],
                                        ps[:, 3 + i % 2, 0:C].rearrange("p (k t) -> p k t", k=KC),
                                        xT[:, 0, :, i * P:(i + 1) * P], ALU.subtract).then_inc(xT_low_ready, 1)

            def rope_in(b, i):
                u = i % 2
                if i >= 2:
                    dve.wait_ge(rope_ready, at(b, NT, i - 1))
                dve.wait_ge(qkv_done, at(b, NT, i + 1))
                dve.wait_ge(qk_copied, at(b, NT, i + 1))
                for w in range(2):
                    ins = nc.vector.tensor_tensor(
                        qk_cos[:, u, w * C:(w + 1) * C].rearrange("p (h d) -> p h d", d=D),
                        ps[:, 1 + u, w * C:(w + 1) * C].rearrange("p (h d) -> p h d", d=D),
                        cos[:, i, w:w + 1, :].to_broadcast([P, H, D]), ALU.mult)
                ins.then_inc(cos_ready, 1)
                dve.wait_ge(sq_ready, at(b, NT, i + 1))
                nc.vector.tensor_reduce(qk_ss[:, u, :], qk_sq[:, u, :].rearrange("p (g d) -> p g d", d=D),
                                        AX_X, ALU.add).then_inc(ss_ready, 1)

            def rope_inverse(b, i):
                u = i % 2
                dve.wait_ge(root_ready, at(b, NT, i + 1))
                link(nc.vector.tensor_scalar(qk_ss[:, u, :], qk_ss[:, u, :], 1e-6, None, ALU.add),
                     "front", front_step, b, FRONT)
                link(nc.vector.reciprocal(qk_ss[:, u, :], qk_ss[:, u, :]), "front", front_step, b, FRONT)

            def rope_norm(b, i):
                u = i % 2
                dve.wait_ge(rope_ready, at(b, NT, i + 1))
                nc.vector.tensor_tensor(qk_sin[:, u, :].rearrange("p (g d) -> p g d", d=D),
                                        qk_cos[:, u, :].rearrange("p (g d) -> p g d", d=D),
                                        qk_ss[:, u, :].unsqueeze(2).to_broadcast([P, 2 * H, D]),
                                        ALU.mult).then_inc(normed, 1)

            def aug_low(b, i):
                u = i % 2
                dve.wait_ge(aug_hi, at(b, NT, i + 1))
                for w, c in ((0, 16), (1, 33)):
                    ins = nc.vector.tensor_tensor(
                        aug[:, u, w, :, c:c + D],
                        qk_sin[:, u, w * C:(w + 1) * C].rearrange("p (h d) -> p h d", d=D),
                        aug[:, u, w, :, 0:D], ALU.subtract)
                ins.then_inc(aug_ready, 1)

            def query_T(b, i):
                dve.wait_ge(augT_done, at(b, NT, i + 1))
                t = half(6).rearrange("p (h t) -> p h t", t=P)
                for par in range(2):
                    r = slice(64 * par, 64 * par + 64)
                    ins = nc.vector.tensor_copy(QT[r, par::2, i * P:(i + 1) * P], t[r])
                ins.then_inc(qt_ready, 1)

            def tables():
                dve.wait_ge(tables_in, 3 * 16)
                nc.vector.tensor_tensor(normw[:, 0, :], normw[:, 0, :], normw[:, 1, :], ALU.mult).then_inc(setup_done, 1)
                dve.wait_ge(setup_done, 1)
                nc.vector.tensor_scalar(normw[:, 1, :], normw[:, 0, :], float(D) ** -0.5, None, ALU.mult).then_inc(setup_done, 1)
                dve.wait_ge(setup_done, 2)
                for t in (cos, sin):
                    nc.vector.tensor_tensor(t[:, :, 0, :], t[:, :, 0, :],
                                            normw[:, 1:2, :].to_broadcast([P, NT, D]), ALU.mult).then_inc(setup_done, 1)
                dve.wait_ge(setup_done, 4)

            def router_weights():
                dve.wait_ge(consts_in, CONSTS)
                nc.vector.tensor_copy(gatew_hl[:, 0], gatew[:]).then_inc(setup_done, 1)
                dve.wait_ge(setup_done, 5)
                nc.vector.tensor_tensor(gatew_hl[:, 1], gatew[:], gatew_hl[:, 0], ALU.subtract).then_inc(setup_done, 1)

            def maxima(b, h):
                g, j = h // HG, h % HG
                for r, tiles in enumerate(((3,), (2, 0), (1,))):
                    dve.wait_ge(s1_done, at(b, 3 * H, 3 * h + r + 1))
                    dve.sem_inc(passed, 1)
                    for i in tiles:
                        w = (i + 1) * P
                        c = 384 if i == 0 else 0
                        ins = nc.vector.tensor_tensor_reduce(
                            ps[:, 3 + r, c:c + w], ps[:, 3 + r, c:c + w], mask[:, T - w:T], 1.0, -BIG,
                            ALU.add, ALU.max, mx[:, i, h:h + 1])
                    ins.then_inc(s1_used, 1)
                if j == HG - 1:
                    dve.wait_ge(s1_used, at(b, 3 * H, 3 * h + 3))
                    for par in range(2):
                        ins = nc.vector.tensor_copy(mx16[:, g, :, 2 * par:2 * par + 2],
                                                    mx[:, :, HG * g + par:HG * g + HG:2])
                    ins.then_inc(max_ready, 1)

            def take(b, g):
                dve.wait_ge(pv_done, at(b, NG, g + 1))
                nc.vector.transpose(yT[:], ps[:, 6, :]).then_inc(y_taken, 1)

            def divide(b, g):
                dve.wait_ge(y_taken, at(b, NG, g + 1))
                y = yT[:].rearrange("p (c d) -> p c d", d=2 * D)
                pair = pairT[:].rearrange("p (c d) -> p c d", d=2 * D)
                z = (g % 2) * D
                link(nc.vector.reciprocal(y[:, :, D], y[:, :, D]), "divide", divide_step, b, DIVIDE)
                link(nc.vector.tensor_tensor(pair[:, :, z:z + D], y[:, :, 0:D],
                                             y[:, :, D:D + 1].to_broadcast([P, T // 32, D]), ALU.mult),
                     "divide", divide_step, b, DIVIDE)
                if g % 2 == 1:
                    nc.vector.transpose(yn[:, g // 2, :], pairT[:]).then_inc(yn_ready, 1)

            def residual1(b, i):
                if i == 0:
                    dve.wait_ge(res_loaded, at(b, 16, 16))
                dve.wait_ge(proj_done, at(b, NT, i + 1))
                nc.vector.tensor_tensor(res[:, i, :], res[:, i, :], ps[:, 3 + i % 2, 0:C], ALU.add).then_inc(x1_ready, 1)
                dve.wait_ge(x1_ready, at(b, NT, i + 1))
                moments(res, i, "norm", norm_step, b, NORM, var_ready)

            def norm2(b, i):
                dve.wait_ge(rstd_ready, at(b, 2 * NT, i + 1))
                normalize(xn, res, i, xn2_ready)

            def xT_low(b, j):
                dve.wait_ge(x2T_hi, at(b, NT, j + 1))
                nc.vector.tensor_tensor(xT_lo[:, :, j * P:(j + 1) * P],
                                        ps[:, 6 + j % 2, 0:C].rearrange("p (k t) -> p k t", k=KC),
                                        xT_hi[:, :, j * P:(j + 1) * P], ALU.subtract).then_inc(x2T_lo, 1)

            def activate(b, f):
                dve.wait_ge(gelu_ready, at(b, NF, f + 1))
                if f >= 4:
                    dve.wait_ge(act_lo_ready, at(b, NF, f - 3))
                nc.vector.tensor_tensor(act[:, f % 4, :], ps[:, HIDDEN_BANK[f % 3], :], gelu[:, f % 2, :], ALU.mult).then_inc(act_ready, 1)

            def residual2(b, i):
                dve.wait_ge(out_done, at(b, NT, i + 1))
                nc.vector.tensor_tensor(res[:, i, :], res[:, i, :], ps[:, OUT_BANK[i], 0:C], ALU.add).then_inc(x2_ready, 1)
                dve.wait_ge(x2_ready, at(b, NT, i + 1))
                moments(res, i, "norm", norm_step, b, NORM, var_ready)

            def norm3(b, i):
                dve.wait_ge(rstd_ready, at(b, 2 * NT, NT + i + 1))
                normalize(xn, res, i, xn3_ready)

            def xh_low(b, j):
                dve.wait_ge(xh_hi, at(b, NT, j + 1))
                nc.vector.tensor_tensor(xh[:, j, C:2 * C], xn[:, j, :], xh[:, j, 0:C], ALU.subtract).then_inc(xh_lo, 1)

            def router(b):
                dve.wait_ge(gate_done, at(b, NT, NT))
                nc.vector.tensor_tensor(
                    logits[:, bass.ds(b * NT, NT), :], ps[:, 1, 0:NT * E].rearrange("p (i e) -> p i e", e=E),
                    gateb[:].unsqueeze(1).to_broadcast([P, NT, E]), ALU.add).then_inc(logits_ready, 1)

            def begin(b, before):
                steps["divide"] = 0
                for h in range(0 if before is None else EARLY, H):
                    maxima(b, h)
                    if before is not None and h - EARLY < 2:
                        xh_low(before, h - EARLY + 2)
                    if before is not None and h == HG + 1:
                        router(before)
                    if h == 13:
                        take(b, 0)

            def finish(b, more):
                steps["norm"] = 0
                n = b + 1
                divide(b, 0)
                if more:
                    norm1_begin(n)
                take(b, 1)
                if more:
                    norm1_end(n)
                divide(b, 1)
                if more:
                    for i in range(NT):
                        norm1_low(n, i)
                take(b, 2)
                divide(b, 2)
                if more:
                    if False:
                        for i in range(NT):
                            norm1_low(n, i)
                    rope_in(n, 0)
                take(b, 3)
                divide(b, 3)
                if more:
                    rope_in(n, 1)
                    rope_inverse(n, 0)
                    rope_norm(n, 0)
                    rope_inverse(n, 1)
                residual1(b, 0)
                if more:
                    rope_norm(n, 1)
                residual1(b, 1)
                norm2(b, 0)
                residual1(b, 2)
                norm2(b, 1)
                residual1(b, 3)
                norm2(b, 2)
                xT_low(b, 0)
                norm2(b, 3)
                xT_low(b, 1)
                if more:
                    aug_low(n, 0)
                xT_low(b, 2)
                xT_low(b, 3)
                if more:
                    rope_in(n, 2)
                    if False:
                        aug_low(n, 0)
                    rope_in(n, 3)
                    rope_inverse(n, 2)
                    aug_low(n, 1)
                    rope_norm(n, 2)
                    rope_inverse(n, 3)
                for f in range(NF):
                    activate(b, f)
                    if more:
                        if f == 0:
                            rope_norm(n, 3)
                        if f == 2:
                            query_T(n, 0)
                        if f == 4:
                            aug_low(n, 2)
                        if f == 5:
                            query_T(n, 1)
                        if f == 6:
                            aug_low(n, 3)
                if more:
                    query_T(n, 2)
                residual2(b, 0)
                if more:
                    query_T(n, 3)
                residual2(b, 1)
                norm3(b, 0)
                if more:
                    maxima(n, 0)
                residual2(b, 2)
                norm3(b, 1)
                xh_low(b, 0)
                if more:
                    maxima(n, 1)
                residual2(b, 3)
                norm3(b, 2)
                xh_low(b, 1)
                norm3(b, 3)

            norm1_begin(0)
            norm1_end(0)
            dve.wait_ge(wqkv_high, 1)
            nc.vector.tensor_tensor(wqkv[:, 1], wqkv_in, wqkv[:, 0], ALU.subtract).then_inc(wqkv_low, 1)
            for i in range(NT):
                norm1_low(0, i)
            nc.vector.memset(QT[:], 0.0).then_inc(cleared_queries, 1)
            tables()
            dve.wait_ge(cleared_queries, 1)
            dve.wait_ge(cleared, 4)
            for i in range(NT + 2):
                if i < NT:
                    rope_in(0, i)
                if 1 <= i <= NT:
                    rope_norm(0, i - 1)
                if i < NT:
                    rope_inverse(0, i)
                if 1 <= i <= NT:
                    aug_low(0, i - 1)
                if i >= 2:
                    query_T(0, i - 2)
            router_weights()
            begin(0, None)
            with dve.Fori(0, B - 1) as it:
                finish(it, True)
                begin(it + 1, it)
            finish(B - 1, False)
            xh_low(B - 1, 2)
            xh_low(B - 1, 3)
            router(B - 1)
            dve.wait_ge(logits_ready, B)
            assert steps["front"] == FRONT and steps["norm"] == NORM, steps
            nc.vector.memset(onesh[:], 1.0).then_inc(p1_done, 1)

            routes = [0]

            def step(ins):
                routes[0] += 1
                ins.then_inc(route_step, 1)
                dve.wait_ge(route_step, routes[0])

            every = [P, B * NT, E]
            dve.wait_ge(sig_ready, 1)
            dve.wait_ge(xh_stored, 32 * B)
            for n in range(2):
                step(nc.vector.tensor_reduce(best[:, n, :], sig[:], AX_X, ALU.max))
                step(nc.vector.tensor_tensor(key[:], sig[:], best[:, n, :].unsqueeze(2).to_broadcast(every), ALU.is_equal))
                step(nc.vector.tensor_tensor(key[:], key[:], eights[:].unsqueeze(1).to_broadcast(every), ALU.mult))
                step(nc.vector.tensor_reduce(first[:, n, :], key[:], AX_X, ALU.max))
                step(nc.vector.tensor_tensor(pick[:, n], eights[:].unsqueeze(1).to_broadcast(every),
                                             first[:, n, :].unsqueeze(2).to_broadcast(every), ALU.is_equal))
                if n == 0:
                    step(nc.vector.scalar_tensor_tensor(sig[:].rearrange("p t e -> p (t e)"), pick[:, 0].rearrange("p t e -> p (t e)"), -4.0,
                                                        sig[:].rearrange("p t e -> p (t e)"), ALU.mult, ALU.add))
            nc.vector.tensor_tensor(picked[:], pick[:, 0], pick[:, 1], ALU.add).then_inc(picked_ready, 1)
            step(nc.vector.tensor_tensor(first[:, 0, :], best[:, 0, :], best[:, 1, :], ALU.add))
            step(nc.vector.tensor_scalar(first[:, 0, :], first[:, 0, :], 1e-6, None, ALU.add))
            step(nc.vector.reciprocal(first[:, 0, :], first[:, 0, :]))
            step(nc.vector.tensor_tensor(share[:], best[:], first[:, 0:1, :].to_broadcast([P, 2, B * NT]), ALU.mult))
            dve.wait_ge(bias_in, 32)
            nc.vector.tensor_scalar(sbd[:], sbd[:], 0.1, None, ALU.mult).then_inc(bias_scaled, 1)

            def shared(b, u):
                for f in range(NF):
                    dve.wait_ge(s_gelu_ready, at(b, NF, f + 1))
                    nc.vector.tensor_copy(s_hi[:, f, :], s_gelu[:, f % 2, :]).then_inc(s_hi_ready, 1)
                    dve.wait_ge(s_hi_ready, at(b, NF, f + 1))
                    nc.vector.tensor_tensor(s_lo[:, f, :], s_gelu[:, f % 2, :], s_hi[:, f, :], ALU.subtract).then_inc(s_lo_ready, 1)
                for c in range(PIECES):
                    dve.wait_ge(w_hi_done, at(b, 2 * PIECES, 3 * PIECES + c + 1))
                    q = slice(c * SPLIT, (c + 1) * SPLIT)
                    nc.vector.tensor_tensor(weights[:, 1, 1, bass.ds(b, 1), q], stage[:, 1:2, q],
                                            weights[:, 1, 0, bass.ds(b, 1), q], ALU.subtract).then_inc(w_lo_down_done, 1)
                dve.wait_ge(r_biased, at(b, 1, 1))
                for i in range(NT):
                    dve.wait_ge(s_out_done, at(b, NT, i + 1))
                    nc.vector.scalar_tensor_tensor(r_in[:, u, i, :], ps[:, 3 + i % 2, 0:C], 0.1, r_in[:, u, i, :],
                                                   ALU.mult, ALU.add).then_inc(res_ready, 1)

            shared(0, 0)
            dve.wait_ge(ranks_done, 1)
            step(nc.vector.tensor_scalar(count[:], ps[:, 6, 0:E], float(MB - 1), None, ALU.add))
            step(nc.vector.tensor_copy(count_i[:], count[:]))
            step(nc.vector.tensor_scalar(count_i[:], count_i[:], MB.bit_length() - 1, None, ALU.arith_shift_right))
            step(nc.vector.tensor_copy(blocks[:], count_i[:]))
            step(nc.vector.tensor_copy(last_block[:, 0, :], blocks[:]))
            a = 0
            for d in (1, 2, 4):
                step(nc.vector.tensor_copy(last_block[:, 1 - a, 0:d], last_block[:, a, 0:d]))
                step(nc.vector.tensor_tensor(last_block[:, 1 - a, d:E], last_block[:, a, d:E], last_block[:, a, 0:E - d], ALU.add))
                a = 1 - a
            step(nc.vector.tensor_tensor(before[:], numbers[:].unsqueeze(2).to_broadcast([1, BLOCKS, E]),
                                         last_block[0:1, a:a + 1, :].to_broadcast([1, BLOCKS, E]), ALU.is_ge))
            step(nc.vector.tensor_reduce(block_f[:], before[:], AX_X, ALU.add))
            step(nc.vector.tensor_scalar(block_f[:], block_f[:], float(E - 1), None, ALU.min))
            step(nc.vector.tensor_copy(block_expert[:], block_f[:]))
            step(nc.vector.tensor_tensor(blocks[:], last_block[:, a, :], blocks[:], ALU.subtract))
            step(nc.vector.tensor_scalar(blocks[:], blocks[:], float(MB), None, ALU.mult))
            step(nc.vector.tensor_tensor(pos[:], ps[:, 5, 0:B * NT * E].rearrange("p (t e) -> p t e", e=E),
                                         blocks[:].unsqueeze(1).to_broadcast(every), ALU.add))
            for n in range(2):
                step(nc.vector.tensor_tensor(key[:], pick[:, n], pos[:], ALU.mult))
                step(nc.vector.tensor_reduce(slot_f[:, n, :], key[:], AX_X, ALU.add))
            nc.vector.tensor_copy(slot_u[:], slot_f[:]).then_inc(routed, 1)

            shared(1, 1)
            with dve.Fori(1, B // 2) as it:
                for u in range(2):
                    shared(it * 2 + u, u)

            dve.wait_ge(slotsT_done, 1)
            nc.vector.tensor_scalar(tokens_u[:, 0, :], ps[:, 6, 0:SLOTS // P], float(N - 1), None, ALU.min).then_inc(tokens_ready, 1)
            nc.vector.tensor_copy(tokens_u[:, 1, :], ps[:, 6, 0:SLOTS // P]).then_inc(tokens_ready, 1)
            nc.vector.tensor_copy(slot_share[:], ps[:, 6, P:P + SLOTS // P]).then_inc(tokens_ready, 1)
            dve.wait_ge(tokens_ready, 3)

            def block_in(j):
                dve.wait_ge(xgT_done, at(j, 1, 1))
                nc.vector.tensor_copy(xgT[:].rearrange("p k t -> p (k t)"), half(7)).then_inc(xgT_ready, 1)

            def block_split(j):
                for q in range(NF // 2):
                    dve.wait_ge(m_gelu_ready, at(j, NF, 2 * q + 2))
                    g = m_gelu[:, q % 2]
                    nc.vector.tensor_copy(m_hi[:, 2 * q:2 * q + 2, :], g).then_inc(m_hi_ready, 1)
                    dve.wait_ge(m_hi_ready, at(j, NF // 2, q + 1))
                    nc.vector.tensor_tensor(m_lo[:, 2 * q:2 * q + 2, :], g, m_hi[:, 2 * q:2 * q + 2, :], ALU.subtract).then_inc(m_lo_ready, 1)

            def block_out(j, u, count):
                e = nc.vector.value_load(block_expert[0:1, bass.ds(j, 1)], min_val=0, max_val=E - 1)
                nc.vector.tensor_copy(g_share[:], slot_share[:, bass.ds(j * MT, MT)]).then_inc(g_share_ready, 1)
                dve.wait_ge(m_out_done, at(j, 1, 1))
                if count is not None:
                    dve.wait_ge(added, 16 * MT * count)
                nc.vector.tensor_tensor(m_y[:, u], ps[:, 4 + u, :].rearrange("p (i c) -> p i c", i=MT),
                                        bdn[:, bass.ds(e, 1), :].to_broadcast([P, MT, C]), ALU.add).then_inc(y_sum_ready, 1)
                dve.wait_ge(g_share_ready, at(j, 1, 1))
                dve.wait_ge(y_sum_ready, at(j, 1, 1))
                dve.sem_inc(passed, 1)
                for i in range(MT):
                    ins = nc.vector.tensor_scalar(m_y[:, u, i, :], m_y[:, u, i, :], g_share[:, i:i + 1], None, ALU.mult)
                ins.then_inc(y_out_ready, 1)

            block_in(0)
            block_split(0)
            dve.wait_ge(bdn_loaded, 16)

            def pair(it, first):
                for u in range(2):
                    j = it * 2 + u + 1
                    block_in(j)
                    block_out(j - 1, u, None if first else j - 2)
                    block_split(j)

            pair(0, True)
            with dve.Fori(1, BLOCKS // 2) as it:
                pair(it, False)
            block_out(BLOCKS - 1, 0, BLOCKS - 2)

        @block.scalar
        def _(sc):

            def x_T(b, i):
                sc.wait_ge(tr1_done, at(b, NT, i + 1))
                nc.scalar.copy(xT[:, 0, :, i * P:(i + 1) * P],
                               ps[:, 3 + i % 2, 0:C].rearrange("p (k t) -> p k t", k=KC)).then_inc(xT_ready, 1)

            def qkv_out(b, i, before):
                u = i % 2
                if i >= 2:
                    sc.wait_ge(rope_ready, at(b, NT, i - 1))
                    sc.wait_ge(normed, at(b, NT, i - 1))
                sc.wait_ge(qkv_done, at(b, NT, i + 1))
                nc.scalar.activation(qk_sq[:, u, :], ps[:, 1 + u, :], ACT.Square).then_inc(sq_ready, 1)
                nc.scalar.copy(qk_sb[:, u, :], ps[:, 1 + u, :]).then_inc(qk_copied, 1)
                if i == 0 and before is not None:
                    sc.wait_ge(pv_done, at(before, NG, NG))
                nc.scalar.copy(vaug[:, i, :, 0:D],
                               ps[:, 5, 0:C].rearrange("p (h d) -> p h d", d=D)).then_inc(v_ready, 1)

            def rope_root(b, i):
                u = i % 2
                sc.wait_ge(ss_ready, at(b, NT, i + 1))
                nc.scalar.activation(qk_ss[:, u, :], qk_ss[:, u, :], ACT.Sqrt, scale=1.0 / D).then_inc(root_ready, 1)

            def aug_high(b, i):
                u = i % 2
                sc.wait_ge(normed, at(b, NT, i + 1))
                if i >= 2:
                    sc.wait_ge(augT_done, at(b, NT, i - 1))
                for w, step in ((0, 33), (1, 16)):
                    src = qk_sin[:, u, w * C:(w + 1) * C].rearrange("p (h d) -> p h d", d=D)
                    for c in range(2):
                        ins = nc.scalar.copy(aug[:, u, w, :, step * c:step * c + D], src)
                ins.then_inc(aug_hi, 1)

            def key_T(b, i):
                sc.wait_ge(augT_done, at(b, NT, i + 1))
                nc.scalar.copy(KT[:, :, i * P:(i + 1) * P],
                               half(7).rearrange("p (h t) -> p h t", t=P)).then_inc(kt_ready, 1)

            def maxT(b, g):
                sc.wait_ge(maxT_done, at(b, NG, g + 1))
                nc.scalar.copy(mT[:, g % 2, :], half(7)[0:HG, 0:T]).then_inc(maxT_ready, 1)

            def exponentials(b, h):
                g, j = h // HG, h % HG
                if g >= 2 and j == 0:
                    sc.wait_ge(pv_done, at(b, NG, g - 1))
                for part, (_, lo, hi) in enumerate(PARTS):
                    sc.wait_ge(st_done, at(b, 2 * H, 2 * h + part + 1))
                    nc.scalar.activation(probs[:, g % 2, j, lo:hi],
                                         ps[:, 0:3, :].rearrange("p b c -> p (b c)")[:, lo:hi],
                                         ACT.Exp).then_inc(exp_done, 1)
                if (h + AHEAD) % HG == 0 and h + AHEAD <= H:
                    maxT(b, (h + AHEAD) // HG - 1)

            def norm2_T(b, i):
                sc.wait_ge(tr2_done, at(b, NT, i + 1))
                nc.scalar.copy(xT_hi[:, :, i * P:(i + 1) * P],
                               ps[:, 6 + i % 2, 0:C].rearrange("p (k t) -> p k t", k=KC)).then_inc(x2T_hi, 1)

            def xh_high(b, i):
                sc.wait_ge(xn3_ready, at(b, NT, i + 1))
                nc.scalar.copy(xh[:, i, 0:C], xn[:, i, :]).then_inc(xh_hi, 1)

            def norm3_T(b, i):
                sc.wait_ge(tr3_done, at(b, NT, i + 1))
                nc.scalar.copy(xT3[:, :, i * P:(i + 1) * P],
                               half(2 + 4 * (i % 2))[:, 0:T].rearrange("p (k t) -> p k t", k=2 * KC)).then_inc(xT3_ready, 1)

            def begin(b, before):
                if before is not None:
                    norm3_T(before, 2)
                maxT(b, 0)
                if before is not None:
                    norm3_T(before, 3)
                sc.wait_ge(ctx_loaded, at(b, 32, 32))
                for w in range(2):
                    for c in range(2):
                        nc.scalar.copy(ctx_hi[:, w, c * 1024:(c + 1) * 1024],
                                       ctx_in[:, w, c * 1024:(c + 1) * 1024]).then_inc(ctx_hi_ready, 1)
                for h in range(CUT):
                    exponentials(b, h)

            def finish(b, more):
                n = b + 1
                for h in range(CUT, H):
                    exponentials(b, h)
                if not more:
                    for w in range(2):
                        sc.wait_ge(stage_in[w], 16)
                        for c in range(PIECES):
                            q = slice(c * SPLIT, (c + 1) * SPLIT)
                            nc.scalar.copy(w_shared[:, w, 0, q], ctx_in[:, w, q]).then_inc(w_hi_done, 1)
                if more:
                    for i in range(NT):
                        x_T(n, i)
                    qkv_out(n, 0, b)
                    rope_root(n, 0)
                    qkv_out(n, 1, None)
                    rope_root(n, 1)
                    aug_high(n, 0)
                    qkv_out(n, 2, None)
                norm2_T(b, 0)
                if more:
                    qkv_out(n, 3, None)
                for i in range(1, NT):
                    norm2_T(b, i)
                if more:
                    aug_high(n, 1)
                    rope_root(n, 2)
                    rope_root(n, 3)
                for f in range(NF + 1):
                    if f < NF:
                        sc.wait_ge(h_done, at(b, NF, f + 1))
                        if f >= 2:
                            sc.wait_ge(act_ready, at(b, NF, f - 1))
                        nc.scalar.activation(gelu[:, f % 2, :], ps[:, HIDDEN_BANK[f % 3], :], ACT.Gelu).then_inc(gelu_ready, 1)
                    if f >= 1:
                        sc.wait_ge(act_ready, at(b, NF, f))
                        nc.scalar.copy(act_hi[:, f - 1, :], act[:, (f - 1) % 4, :]).then_inc(act_hi_ready, 1)
                    if more:
                        if f == 2:
                            key_T(n, 0)
                        if f == 3:
                            aug_high(n, 2)
                        if f == 5:
                            key_T(n, 1)
                            aug_high(n, 3)
                if more:
                    key_T(n, 2)
                    key_T(n, 3)
                for i in range(3):
                    xh_high(b, i)
                norm3_T(b, 0)
                xh_high(b, 3)
                norm3_T(b, 1)

            sc.wait_ge(first_in, 32)
            nc.scalar.copy(wqkv[:, 0], wqkv_in).then_inc(wqkv_high, 1)
            for i in range(NT):
                x_T(0, i)
            sc.wait_ge(cleared, 4)
            for i in range(NT + 2):
                if i < NT:
                    qkv_out(0, i, None)
                    rope_root(0, i)
                if 1 <= i <= NT:
                    aug_high(0, i - 1)
                if i >= 2:
                    key_T(0, i - 2)
            begin(0, None)
            with sc.Fori(0, B - 1) as it:
                finish(it, True)
                begin(it + 1, it)
            finish(B - 1, False)
            norm3_T(B - 1, 2)
            norm3_T(B - 1, 3)

            sc.wait_ge(p1_done, 1)
            nc.scalar.activation(sig[:], logits[:], ACT.Sigmoid).then_inc(sig_ready, 1)
            sc.wait_ge(bias_in, 32)

            def shared(b):
                for f in range(NF):
                    sc.wait_ge(sh_done, at(b, NF, f + 1))
                    if f >= 2:
                        sc.wait_ge(s_lo_ready, at(b, NF, f - 1))
                    nc.scalar.activation(s_gelu[:, f % 2, :], ps[:, f % 3, :], ACT.Gelu,
                                         bias=bup[:, E, f:f + 1]).then_inc(s_gelu_ready, 1)
                    w, c = f // PIECES, f % PIECES
                    if c == 0:
                        sc.wait_ge(stage_in[w], at(b, 16, 32))
                    q = slice(c * SPLIT, (c + 1) * SPLIT)
                    nc.scalar.copy(weights[:, w, 0, bass.ds(b, 1), q], stage[:, w:w + 1, q]).then_inc(w_hi_done, 1)

            shared(0)
            shared(1)
            with sc.Fori(1, B // 2) as it:
                for u in range(2):
                    shared(it * 2 + u)

            def block_gelu(j):
                e = nc.scalar.value_load(block_expert[0:1, bass.ds(j, 1)], min_val=0, max_val=E - 1)
                for f in range(NF):
                    q = f // 2
                    if f % 2 == 0:
                        sc.wait_ge(mh_done, at(j, NF // 2, q + 1))
                    if q >= 2 and f % 2 == 0:
                        sc.wait_ge(m_lo_ready, at(j, NF // 2, q - 1))
                    sc.sem_inc(passed, 1)
                    nc.scalar.activation(m_gelu[:, q % 2, f % 2, :], ps[:, q, (f % 2) * MB:(f % 2 + 1) * MB], ACT.Gelu,
                                         bias=bup[:, bass.ds(e, 1), f:f + 1].rearrange("p o n -> p (o n)")).then_inc(m_gelu_ready, 1)

            block_gelu(0)
            with sc.Fori(0, BLOCKS // 2) as it:
                for u in range(2):
                    block_gelu(it * 2 + u + 1)

        @block.gpsimd
        def _(pool):
            nc.gpsimd.memset(minus_half[:], -0.5).then_inc(cleared, 1)
            nc.gpsimd.memset(aug[:], 0.0).then_inc(cleared, 1)
            pool.wait_ge(cleared, 2)
            nc.gpsimd.memset(aug[:, :, 1, :, 32:33], -1.0).then_inc(cleared, 1)

            def inverse_root(i, var, count, ready):
                pool.wait_ge(var, count)
                nc.gpsimd.tensor_tensor(rstd[:, i:i + 1], mv[:, i, 1:2], minus_half[:], ALU.pow).then_inc(ready, 1)

            def root1(b, i):
                inverse_root(i, var1_ready, at(b, NT, i + 1), rstd1_ready)

            def root2(b, i):
                inverse_root(i, var_ready, at(b, 2 * NT, i + 1), rstd_ready)

            def root3(b, i):
                inverse_root(i, var_ready, at(b, 2 * NT, NT + i + 1), rstd_ready)

            def rope_sum(b, i):
                u = i % 2
                pool.wait_ge(qk_copied, at(b, NT, i + 1))
                if i >= 2:
                    pool.wait_ge(aug_ready, at(b, NT, i - 1))
                a = qk_sb[:, u, :].rearrange("p (w h d) -> p w h d", w=2, d=D)
                o = qk_sin[:, u, :].rearrange("p (w h d) -> p w h d", w=2, d=D)
                for w in range(2):
                    for z in range(2):
                        to, fr = slice(8 * z, 8 * z + 8), slice(8 - 8 * z, 16 - 8 * z)
                        ins = nc.gpsimd.tensor_tensor(o[:, w, :, to], a[:, w, :, fr],
                                                      sin[:, i, w:w + 1, to].to_broadcast([P, H, 8]), ALU.mult)
                ins.then_inc(pool_step, 1)
                pool.wait_ge(pool_step, at(b, NT, i + 1))
                pool.wait_ge(cos_ready, at(b, NT, i + 1))
                nc.gpsimd.tensor_tensor(qk_cos[:, u, :], qk_cos[:, u, :], qk_sin[:, u, :], ALU.add).then_inc(rope_ready, 1)

            def causal(b, h):
                g, j = h // HG, h % HG
                for part, (tiles, _, _) in enumerate(PARTS):
                    pool.wait_ge(exp_done, at(b, 2 * H, 2 * h + part + 1))
                    pool.sem_inc(passed, 1)
                    for s in tiles:
                        v = probs[:, g % 2, j, PT_AT[s]:PT_AT[s] + P]
                        ins = nc.gpsimd.affine_select(out=v, in_=v, compare_op=ALU.is_ge,
                                                      fill=0.0, base=0, pattern=[[1, P]], channel_multiplier=-1)
                ins.then_inc(causal_done, 1)

            def split_shared(w):
                for c in range(PIECES):
                    pool.wait_ge(w_hi_done, PIECES * w + c + 1)
                    q = slice(c * SPLIT, (c + 1) * SPLIT)
                    nc.gpsimd.tensor_tensor(w_shared[:, w, 1, q], ctx_in[:, w, q], w_shared[:, w, 0, q], ALU.subtract).then_inc(w_lo_done, 1)

            def begin(b):
                for w in range(2):
                    for c in range(4):
                        pool.wait_ge(ctx_hi_ready, at(b, 4, 2 * w + c // 2 + 1))
                        q = slice(c * 512, (c + 1) * 512)
                        nc.gpsimd.tensor_tensor(ctx_lo[:, w, q], ctx_in[:, w, q], ctx_hi[:, w, q],
                                                ALU.subtract).then_inc(ctx_lo_ready, 1)
                for h in range(CUT):
                    causal(b, h)

            def finish(b, more):
                n = b + 1
                for h in range(CUT, H):
                    causal(b, h)
                    if more and h < CUT + 2:
                        root1(n, 2 * (h - CUT))
                        root1(n, 2 * (h - CUT) + 1)
                if not more:
                    split_shared(0)
                if more:
                    rope_sum(n, 0)
                    rope_sum(n, 1)
                for i in range(NT):
                    root2(b, i)
                if more:
                    rope_sum(n, 2)
                    rope_sum(n, 3)
                for f in range(NF):
                    pool.wait_ge(act_hi_ready, at(b, NF, f + 1))
                    nc.gpsimd.tensor_tensor(act_lo[:, f, :], act[:, f % 4, :], act_hi[:, f, :],
                                            ALU.subtract).then_inc(act_lo_ready, 1)
                for i in range(NT):
                    root3(b, i)
                if not more:
                    split_shared(1)

            for i in range(NT):
                root1(0, i)
            nc.gpsimd.memset(vaug[:], 1.0).then_inc(cleared, 1)
            pool.wait_ge(setup_done, 4)
            for i in range(NT):
                rope_sum(0, i)
            begin(0)
            with pool.Fori(0, B - 1) as it:
                finish(it, True)
                begin(it + 1)
            finish(B - 1, False)


            def scatter_in(b):
                nc.gpsimd.tensor_copy(sc_slot[:], slot_u[:, :, bass.ds(b * NT, NT)]).then_inc(slots_copied, 1)
                nc.gpsimd.tensor_copy(sc_token[:, :, :, 0], token_id[:, bass.ds(b * NT, NT)].unsqueeze(2).to_broadcast([P, NT, 2])
                                      ).then_inc(slots_copied, 1)
                nc.gpsimd.tensor_copy(sc_token[:, :, :, 1].rearrange("p i n -> p n i"), share[:, :, bass.ds(b * NT, NT)]
                                      ).then_inc(slots_copied, 1)
                pool.wait_ge(slots_copied, at(b, 3, 3))
                pool.sem_inc(passed, 1)

            def scatter(m):
                i, n = m // 2, m % 2
                nc.gpsimd.indirect_dma_start(slot_dram, bass.IndirectOffsetOnAxis(sc_slot[:, n, i:i + 1], 0),
                                             sc_token[:, i, n, :], None).then_inc(tokens_put, 16)

            def scattered(b):
                pool.wait_ge(tokens_put, at(b, 16 * 2 * NT, 16 * 2 * NT))
                pool.sem_inc(passed, 1)

            def split_up(b, c):
                pool.wait_ge(w_hi_done, at(b, 2 * PIECES, 2 * PIECES + c + 1))
                q = slice(c * SPLIT, (c + 1) * SPLIT)
                nc.gpsimd.tensor_tensor(weights[:, 0, 1, bass.ds(b, 1), q], stage[:, 0:1, q],
                                        weights[:, 0, 0, bass.ds(b, 1), q], ALU.subtract).then_inc(w_lo_done, 1)

            def add_bias(u, round):
                pool.wait_ge(r_loaded[u], at(round, 16, 16))
                nc.gpsimd.tensor_tensor(r_in[:, u], r_in[:, u], sbd[:].unsqueeze(1).to_broadcast([P, NT, C]), ALU.add).then_inc(r_biased, 1)

            for c in range(PIECES):
                split_up(0, c)
            pool.wait_ge(bias_scaled, 1)
            add_bias(0, 0)
            for c in range(PIECES):
                split_up(1, c)
            pool.wait_ge(routed, 1)
            for b in range(2):
                scatter_in(b)
                for m in range(2 * NT):
                    scatter(m)
                    if b == 0 and m == 2:
                        add_bias(1, 0)
                scattered(b)
            with pool.Fori(1, B // 2) as it:
                for u in range(2):
                    b = it * 2 + u
                    scatter_in(b)
                    for c in range(PIECES):
                        split_up(b, c)
                        if c == 1:
                            add_bias(u, it)
                    for m in range(2 * NT):
                        scatter(m)
                    scattered(b)

            pool.wait_ge(tokens_ready, 3)

            def gather(j, u):
                nc.gpsimd.tensor_copy(g_token[:, u, :], tokens_u[:, 0, bass.ds(j * MT, MT)]).then_inc(g_token_ready, 1)
                pool.wait_ge(g_token_ready, at(j, 1, 1))
                pool.sem_inc(passed, 1)
                for i in range(MT):
                    nc.gpsimd.indirect_dma_start(xg[:, u, i, :], None, xh_dram,
                                                 bass.IndirectOffsetOnAxis(g_token[:, u, i:i + 1], 0)).then_inc(gathered[u], 16)

            def add(j, u):
                nc.gpsimd.tensor_copy(g_dest[:], tokens_u[:, 1, bass.ds(j * MT, MT)]).then_inc(g_dest_ready, 1)
                pool.wait_ge(g_dest_ready, at(j, 1, 1))
                pool.wait_ge(y_out_ready, at(j, 1, 1))
                pool.sem_inc(passed, 1)
                for i in range(MT):
                    nc.gpsimd.indirect_dma_start(res_dram, bass.IndirectOffsetOnAxis(g_dest[:, i:i + 1], 0),
                                                 m_y[:, u, i, :], None, compute_op=ALU.add).then_inc(added, 16)
                pool.wait_ge(added, at(j, 16 * MT, 16 * MT))
                pool.sem_inc(passed, 1)

            gather(0, 0)
            gather(1, 1)
            with pool.Fori(0, BLOCKS // 2 - 1) as it:
                for u in range(2):
                    j = it * 2 + u
                    pool.wait_ge(xgT_done, at(j, 1, 1))
                    gather(j + 2, u)
                    add(j, u)
            pool.wait_ge(xgT_done, BLOCKS - 2)
            gather(BLOCKS - 1, 0)
            for j in (BLOCKS - 3, BLOCKS - 2, BLOCKS - 1):
                add(j, j % 2)

        @block.tensor
        def _(pe):
            pe.wait_ge(first_in, 32)

            def tr1(b, i):
                pe.wait_ge(xn1_ready, at(b, NT, i + 1))
                if i >= 2:
                    pe.wait_ge(xT_low_ready, at(b, NT, i - 1))
                for k in range(KC):
                    ins = nc.tensor.transpose(ps[:, 3 + i % 2, k * P:(k + 1) * P], xn1[:, i, k * P:(k + 1) * P], ident[:])
                ins.then_inc(tr1_done, 1)

            def qkv(b, i):
                u = i % 2
                pe.wait_ge(xT_low_ready, at(b, NT, i + 1))
                if i >= 2:
                    pe.wait_ge(cos_ready, at(b, NT, i - 1))

                def product(dst, cols):
                    n = 0
                    for k in range(KC):
                        for a, w in ((0, 0), (0, 1), (1, 0)):
                            ins = nc.tensor.matmul(dst, xT[:, a, k, i * P:(i + 1) * P], wqkv[:, w, k, cols],
                                                   start=(n == 0), stop=(n == 5))
                            n += 1
                    return ins

                product(ps[:, 1 + u, :], slice(0, 2 * C))
                if i >= 1:
                    pe.wait_ge(v_ready, at(b, NT, i))
                product(ps[:, 5, 0:C], slice(2 * C, 3 * C)).then_inc(qkv_done, 1)

            def augT(b, i):
                pe.wait_ge(aug_ready, at(b, NT, i + 1))
                if i >= 1:
                    pe.wait_ge(qt_ready, at(b, NT, i))
                    pe.wait_ge(kt_ready, at(b, NT, i))
                for w in range(2):
                    for q in range(H // 2):
                        ins = nc.tensor.transpose(half(6 + w)[:, q * P:(q + 1) * P],
                                                  aug[:, i % 2, w, 2 * q:2 * q + 2, :].rearrange("p h c -> p (h c)"), identh[:])
                ins.then_inc(augT_done, 1)

            def scores(b, h):
                for r, tiles in enumerate(((3,), (2, 0), (1,))):
                    if h >= 1:
                        pe.wait_ge(s1_used, at(b, 3 * H, 3 * (h - 1) + r + 1))
                    for i in tiles:
                        w = (i + 1) * P
                        c = 384 if i == 0 else 0
                        ins = nc.tensor.matmul(ps[:, 3 + r, c:c + w], QT[:, h, i * P:(i + 1) * P], KT[:, h // 2, 0:w],
                                               start=True, stop=True)
                    ins.then_inc(s1_done, 1)

            def maxT(b, g):
                pe.wait_ge(max_ready, at(b, NG, g + 1))
                if g >= 1:
                    pe.wait_ge(maxT_ready, at(b, NG, g))
                for i in range(NT):
                    ins = nc.tensor.transpose(half(7)[0:HG, i * P:(i + 1) * P], mx16[:, g, i, :], identh[:])
                ins.then_inc(maxT_done, 1)

            def scoresT(b, h):
                if h % HG == 0:
                    pe.wait_ge(max_rows, at(b, 32 * NG, 32 * (h // HG + 1)))
                flat = ps[:, 0:3, :].rearrange("p b c -> p (b c)")
                for part, (tiles, _, _) in enumerate(PARTS):
                    if h >= 1:
                        pe.wait_ge(exp_done, at(b, 2 * H, 2 * (h - 1) + part + 1))
                    for s in tiles:
                        c, w = PT_AT[s], T - s * P
                        ins = nc.tensor.matmul(flat[:, c:c + w], KT[:, h // 2, s * P:(s + 1) * P], QT[:, h, s * P:T],
                                               start=True, stop=True)
                    ins.then_inc(st_done, 1)

            def values(b, g):
                pe.wait_ge(causal_done, at(b, H, HG * (g + 1)))
                if g >= 1:
                    pe.wait_ge(y_taken, at(b, NG, g))
                for s in range(NT):
                    c, w = PT_AT[s], T - s * P
                    for j in range(HG):
                        ins = nc.tensor.matmul(ps[32 * j:32 * j + 32, 6, s * P:T], vaug[:, s, HG * g + j, :],
                                               probs[:, g % 2, j, c:c + w], start=(s == 0), stop=(s == NT - 1))
                ins.then_inc(pv_done, 1)

            def project(b, i):
                if i == 0:
                    pe.wait_ge(yn_ready, at(b, NG // 2, NG // 2))
                if i >= 2:
                    pe.wait_ge(x1_ready, at(b, NT, i - 1))
                for q in range(NG // 2):
                    ins = nc.tensor.matmul(ps[:, 3 + i % 2, 0:C], yn[:, q, i * P:(i + 1) * P], wproj[:, q, :],
                                           start=(q == 0), stop=(q == NG // 2 - 1))
                ins.then_inc(proj_done, 1)

            def tr2(b, i):
                pe.wait_ge(xn2_ready, at(b, NT, i + 1))
                if i >= 2:
                    pe.wait_ge(x2T_lo, at(b, NT, i - 1))
                for k in range(KC):
                    ins = nc.tensor.transpose(ps[:, 6 + i % 2, k * P:(k + 1) * P], xn[:, i, k * P:(k + 1) * P], ident[:])
                ins.then_inc(tr2_done, 1)

            def hidden(b, f):
                if f == 0:
                    pe.wait_ge(x2T_lo, at(b, NT, NT))
                    pe.wait_ge(ctx_lo_ready, at(b, 8, 8))
                if f >= 3:
                    pe.wait_ge(act_ready, at(b, NF, f - 2))
                n = 0
                for k in range(KC):
                    for w, a in ((ctx_cols[0], xT_hi), (ctx_cols[0], xT_lo), (ctx_cols[1], xT_hi)):
                        ins = nc.tensor.matmul(ps[:, HIDDEN_BANK[f % 3], :], w[:, k, f * P:(f + 1) * P], a[:, k, :],
                                               start=(n == 0), stop=(n == 5))
                        n += 1
                ins.then_inc(h_done, 1)

            def xout(b, i, more=False):
                if i == 0 and more:
                    pe.wait_ge(cos_ready, at(b + 1, NT, NT))
                if i == 3:
                    pe.wait_ge(x2_ready, at(b, NT, 1))
                for f in range(NF):
                    if i == 0:
                        pe.wait_ge(act_lo_ready, at(b, NF, f + 1))
                    for n, (a, w) in enumerate(((act_hi, 0), (act_hi, 1), (act_lo, 0))):
                        ins = nc.tensor.matmul(ps[:, OUT_BANK[i], 0:C], a[:, f, i * P:(i + 1) * P], ctx_rows[w][:, f, :],
                                               start=(f == 0 and n == 0), stop=(f == NF - 1 and n == 2))
                ins.then_inc(out_done, 1)

            def tr3(b, i):
                pe.wait_ge(xh_lo, at(b, NT, i + 1))
                if i >= 2:
                    pe.wait_ge(xT3_ready, at(b, NT, i - 1))
                for k in range(2 * KC):
                    ins = nc.tensor.transpose(half(2 + 4 * (i % 2))[:, k * P:(k + 1) * P], xh[:, i, k * P:(k + 1) * P], identh[:])
                ins.then_inc(tr3_done, 1)

            def gate(b):
                for i in range(NT):
                    pe.wait_ge(xT3_ready, at(b, NT, i + 1))
                    n = 0
                    for k in range(KC):
                        for a, w in ((k, 0), (k, 1), (KC + k, 0)):
                            ins = nc.tensor.matmul(ps[:, 1, i * E:(i + 1) * E], xT3[:, a, i * P:(i + 1) * P], gatew_hl[:, w, k, :],
                                                   start=(n == 0), stop=(n == 5))
                            n += 1
                    ins.then_inc(gate_done, 1)

            def transposed(b, h):
                scoresT(b, h)
                if h + AHEAD < H:
                    scores(b, h + AHEAD)
                if (h + AHEAD) % HG == 0 and h + AHEAD <= H:
                    maxT(b, (h + AHEAD) // HG - 1)
                if h % HG == 2 and h >= HG:
                    values(b, h // HG - 1)

            def ready(b):
                pe.wait_ge(qt_ready, at(b, NT, NT))
                pe.wait_ge(kt_ready, at(b, NT, NT))
                pe.wait_ge(v_ready, at(b, NT, NT))

            def begin(b, before):
                if before is None:
                    ready(b)
                for h in range(0 if before is None else EARLY + 1, AHEAD):
                    scores(b, h)
                    if before is not None and h == EARLY + 1:
                        tr3(before, 2)
                    if h == HG:
                        maxT(b, 0)
                        if before is not None:
                            tr3(before, 3)
                            gate(before)
                if before is None:
                    pe.wait_ge(setup_done, 6)
                else:
                    pe.wait_ge(logits_ready, at(before, 1, 1))
                for h in range(CUT):
                    transposed(b, h)

            def finish(b, more):
                n = b + 1
                for h in range(CUT, H):
                    transposed(b, h)
                if more:
                    for i in range(NT):
                        tr1(n, i)
                    pe.wait_ge(exp_done, at(b, 2 * H, 2 * H))
                    qkv(n, 0)
                values(b, NG - 1)
                if more:
                    qkv(n, 1)
                project(b, 0)
                project(b, 1)
                if more:
                    qkv(n, 2)
                project(b, 2)
                project(b, 3)
                if more:
                    qkv(n, 3)
                for i in range(NT):
                    tr2(b, i)
                for f in range(NF):
                    hidden(b, f)
                    if more and f % 3 == 1:
                        augT(n, f // 3)
                xout(b, 0, more)
                if more:
                    augT(n, 3)
                xout(b, 1)
                if more:
                    ready(n)
                    scores(n, 0)
                xout(b, 2)
                if more:
                    scores(n, 1)
                xout(b, 3)
                if more:
                    scores(n, 2)
                tr3(b, 0)
                tr3(b, 1)

            for i in range(NT):
                tr1(0, i)
            pe.wait_ge(wqkv_low, 1)
            for i in range(NT):
                qkv(0, i)
            pe.wait_ge(consts_in, CONSTS)
            for i in range(NT):
                augT(0, i)
            begin(0, None)
            with pe.Fori(0, B - 1) as it:
                finish(it, True)
                begin(it + 1, it)
            finish(B - 1, False)
            tr3(B - 1, 2)
            tr3(B - 1, 3)
            gate(B - 1)

            up = [w_shared[:, 0, n].rearrange("p (k f) -> p k f", k=KC) for n in range(2)]
            down = [w_shared[:, 1, n].rearrange("p (f c) -> p f c", f=NF) for n in range(2)]

            def shared(b, u, round):
                pe.wait_ge(xt_loaded[u], at(round, 16, 16))
                for f in range(NF):
                    if f >= 3:
                        pe.wait_ge(s_gelu_ready, at(b, NF, f - 2))
                    n = 0
                    for k in range(KC):
                        for w, a in ((0, k), (0, KC + k), (1, k)):
                            ins = nc.tensor.matmul(ps[:, f % 3, :], up[w][:, k, f * P:(f + 1) * P], xt_in[:, u, a, :],
                                                   start=(n == 0), stop=(n == 5))
                            n += 1
                    ins.then_inc(sh_done, 1)
                for i in range(NT):
                    if i >= 2:
                        pe.wait_ge(res_ready, at(b, NT, i - 1))
                    for f in range(NF):
                        if i == 0:
                            pe.wait_ge(s_lo_ready, at(b, NF, f + 1))
                        for n, (a, w) in enumerate(((s_hi, 0), (s_hi, 1), (s_lo, 0))):
                            ins = nc.tensor.matmul(ps[:, 3 + i % 2, 0:C], a[:, f, i * P:(i + 1) * P], down[w][:, f, :],
                                                   start=(f == 0 and n == 0), stop=(f == NF - 1 and n == 2))
                    ins.then_inc(s_out_done, 1)

            pe.wait_ge(w_lo_done, 2 * PIECES)
            pe.wait_ge(logits_ready, B)
            shared(0, 0, 0)

            pe.wait_ge(picked_ready, 1)
            flat = picked[:].rearrange("p t e -> p (t e)")
            nc.tensor.matmul(ps[:, 5, 0:B * NT * E], upper[:], flat, start=True, stop=False, skip_group_check=True)
            for d in range(1, B * NT):
                nc.tensor.matmul(ps[:, 5, d * E:B * NT * E], onesh[:], flat[:, 0:(B * NT - d) * E],
                                 start=False, stop=(d == B * NT - 1), skip_group_check=True)
            for t in range(B * NT):
                ins = nc.tensor.matmul(ps[:, 6, 0:E], onesh[:], flat[:, t * E:(t + 1) * E], start=(t == 0), stop=(t == B * NT - 1))
            ins.then_inc(ranks_done, 1)

            shared(1, 1, 0)
            with pe.Fori(1, B // 2) as it:
                for u in range(2):
                    shared(it * 2 + u, u, it)

            pe.wait_ge(slots_loaded, 16)
            for n in range(2):
                ins = nc.tensor.transpose(ps[:, 6, n * P:n * P + SLOTS // P], slot_rows[:, :, n], ident[0:SLOTS // P, 0:SLOTS // P])
            ins.then_inc(slotsT_done, 1)
            pe.wait_ge(w_lo_done, PIECES * (E + 2))
            pe.wait_ge(w_lo_down_done, PIECES * E)

            def block_T(j, u, count):
                pe.wait_ge(gathered[u], count)
                pe.sem_inc(passed, 1)
                for k in range(2 * KC):
                    for i in range(MT):
                        ins = nc.tensor.transpose(half(7)[:, (k * MT + i) * P:(k * MT + i + 1) * P],
                                                  xg[:, u, i, k * P:(k + 1) * P], identh[:])
                ins.then_inc(xgT_done, 1)

            def block_up(j, e):
                pe.wait_ge(xgT_ready, at(j, 1, 1))
                pe.sem_inc(passed, 1)
                for f in range(NF):
                    n = 0
                    for k in range(KC):
                        for w, a in ((0, k), (0, KC + k), (1, k)):
                            c = k * F + f * P
                            ins = nc.tensor.matmul(ps[:, f // 2, (f % 2) * MB:(f % 2 + 1) * MB],
                                                   weights[:, 0, w, bass.ds(e, 1), c:c + P].rearrange("p o n -> p (o n)"),
                                                   xgT[:, a, :], start=(n == 0), stop=(n == 5), skip_group_check=True)
                            n += 1
                    if f % 2 == 1:
                        ins.then_inc(mh_done, 1)

            def block_down(j, e, u):
                for i in range(MT):
                    for f in range(NF):
                        if i == 0 and f % 2 == 0:
                            pe.wait_ge(m_lo_ready, at(j, NF // 2, f // 2 + 1))
                            pe.sem_inc(passed, 1)
                        for n, (a, w) in enumerate(((m_hi, 0), (m_hi, 1), (m_lo, 0))):
                            ins = nc.tensor.matmul(ps[:, 4 + u, i * C:(i + 1) * C], a[:, f, i * P:(i + 1) * P],
                                                   weights[:, 1, w, bass.ds(e, 1), f * C:(f + 1) * C].rearrange("p o n -> p (o n)"),
                                                   start=(f == 0 and n == 0), stop=(f == NF - 1 and n == 2), skip_group_check=True)
                ins.then_inc(m_out_done, 1)

            def expert(j):
                return nc.tensor.value_load(block_expert[0:1, bass.ds(j, 1)], min_val=0, max_val=E - 1)

            block_T(0, 0, 32)
            block_up(0, expert(0))
            with pe.Fori(0, BLOCKS // 2) as it:
                for u in range(2):
                    j = it * 2 + u + 1
                    block_T(j, 1 - u, at(it, 32, 32 + 32 * u))
                    block_down(j - 1, expert(j - 1), u)
                    block_up(j, expert(j))
            block_down(BLOCKS - 1, expert(BLOCKS - 1), 0)


def layouts(inp):
    f = np.float32
    a = {k: np.asarray(v) for k, v in inp.items()}
    w = a["L0_attn_W_kqv"]
    w_qkv = np.concatenate([w[C:2 * C], w[0:C], w[2 * C:3 * C]], 0)
    pos = np.arange(T, dtype=f)
    inv = (1.0 / np.float32(10000.0) ** (np.arange(0, D, 2, dtype=f) / np.float32(D))).astype(f)
    fr = (pos[:, None] * inv[None, :]).astype(f)
    cos = np.cos(np.concatenate([fr, fr], -1)).astype(f).reshape(NT, P, 1, D).transpose(1, 0, 2, 3)
    sin = np.sin(np.concatenate([-fr, fr], -1)).astype(f).reshape(NT, P, 1, D).transpose(1, 0, 2, 3)
    tri = np.where(np.arange(P)[None, :] > np.arange(P)[:, None], -BIG / 10, 0.0).astype(f)
    return {
        "x": a["x"],
        "ctx": a["ctx_1024"],
        "ctxT": a["ctx_1024"].transpose(0, 2, 1),
        "wqkv": w_qkv.T.reshape(KC, P, 3 * C).transpose(1, 0, 2),
        "wproj": a["L0_attn_W_proj"].T.reshape(NG // 2, 2, HG, D, C).transpose(2, 1, 3, 0, 4).reshape(P, NG // 2, C),
        "normw": np.broadcast_to(np.stack([a["L0_attn_q_norm_w"], a["L0_attn_k_norm_w"]]), (P, 2, D)),
        "cos": np.broadcast_to(cos, (P, NT, 2, D)),
        "sin": np.broadcast_to(sin, (P, NT, 2, D)),
        "mask": np.concatenate([np.zeros((P, T - P), f), tri], 1),
        "ident": np.eye(P, dtype=f),
        "identh": np.eye(P, dtype=np.float16),
        "gatew": a["L0_ffn_gate_w"].T.reshape(KC, P, E).transpose(1, 0, 2),
        "gateb": np.broadcast_to(a["L0_ffn_gate_bias"], (P, E)),
        "upper": np.triu(np.ones((P, P), np.float16), 1),
        "eights": np.broadcast_to(np.arange(E, 0, -1, dtype=f), (P, E)),
        "padding": np.stack([N + np.arange(SLOTS, dtype=f) % MB, np.zeros(SLOTS, f)], 1),
        "numbers": np.arange(BLOCKS, dtype=f)[None],
        "token_id": np.arange(N, dtype=f).reshape(B * NT, P).T,
        "swu": a["L0_ffn_sWu"].T.reshape(KC, P, F).transpose(1, 0, 2).reshape(P, KC * F),
        "swd": a["L0_ffn_sWd"].T.reshape(NF, P, C).transpose(1, 0, 2).reshape(P, NF * C),
        "wu": a["L0_ffn_Wu"].transpose(0, 2, 1).reshape(E, KC, P, F).transpose(0, 2, 1, 3).reshape(E, P, KC * F),
        "wd": a["L0_ffn_Wd"].transpose(0, 2, 1).reshape(E, NF, P, C).transpose(0, 2, 1, 3).reshape(E, P, NF * C),
        "bup": np.concatenate([a["L0_ffn_bu"], a["L0_ffn_sbu"][None]], 0).reshape(E + 1, NF, P).transpose(2, 0, 1),
        "sbd": np.broadcast_to(a["L0_ffn_sbd"], (P, C)),
        "bdn": np.broadcast_to(a["L0_ffn_bd"], (P, E, C)),
    }


def kernel(**inputs):
    import numpy as _np
    import concourse.bacc as _bacc
    from concourse import mybir as _mybir
    from concourse.bass_utils import run_bass_kernel_spmd as _run

    nc = _bacc.Bacc("TRN2", target_bir_lowering=False, num_devices=1)
    arrays, args = {}, {}
    for name, a in layouts(inputs).items():
        a = _np.ascontiguousarray(a)
        arrays[f"in_{name}"] = a
        args[name] = nc.dram_tensor(f"in_{name}", a.shape, _mybir.dt.from_np(a.dtype), kind="ExternalInput").ap()
    out = nc.dram_tensor("out_0", (B, T, C), _mybir.dt.float32, kind="ExternalOutput").ap()
    decoder_kernel(nc, args, out)
    r = _run(nc, [arrays], core_ids=[0])
    return r.results[0]["out_0"]
```
